# Optimizing a Trainium2 kernel written in Bass

```python
import numpy as np
import jax
import jax.numpy as jnp

def _softmax(x, axis=-1):
    return jax.nn.softmax(x, axis=axis)

def _gelu(x):
    return jax.nn.gelu(x, approximate=True)

def _silu(x):
    return jax.nn.silu(x)

def _sigmoid(x):
    return jax.nn.sigmoid(x)

def _layernorm(x, axis=-1, eps=1e-05):
    m = jnp.mean(x, axis=axis, keepdims=True)
    v = jnp.var(x, axis=axis, keepdims=True)
    return (x - m) / jnp.sqrt(v + eps)

def _scatter_add(tgt, idx, src, axis=0):
    return tgt.at[idx].add(src)

def _segment_sum(src, seg, n):
    return jax.ops.segment_sum(src, seg, n)
kernel_name = 'mk_recurrent_d1_jaxref_r8_2ecb94'

def setup_inputs(seed: int=0):
    np.random.seed(seed)
    _w = jnp.asarray

    def _L0_attn_setup():
        import jax, jax.numpy as jnp
        import numpy as np
        ROPE_THETA = 10000.0
        NH, D_NOPE, D_ROPE, D_V = (16, 128, 64, 128)
        D_QK = D_NOPE + D_ROPE
        KV_LORA = 64
        SCALING = D_QK ** (-0.5)
        EPS = 1e-06

        def rmsnorm(x, w):
            xf = x.astype(jnp.float32)
            var = jnp.mean(xf * xf, axis=-1, keepdims=True)
            return (w * (xf * jax.lax.rsqrt(var + EPS))).astype(x.dtype)

        def rotate_half(x):
            x1, x2 = jnp.split(x, 2, axis=-1)
            return jnp.concatenate([-x2, x1], axis=-1)

        def rope_cos_sin(seq_len, dim, dtype):
            inv_freq = 1.0 / ROPE_THETA ** (jnp.arange(0, dim, 2, dtype=jnp.float32) / dim)
            t = jnp.arange(seq_len, dtype=jnp.float32)
            ang = jnp.outer(t, inv_freq)
            emb = jnp.concatenate([ang, ang], axis=-1)
            return (jnp.cos(emb).astype(dtype), jnp.sin(emb).astype(dtype))
        key = jax.random.key(seed)
        ks = jax.random.split(key, 8)
        B, S, H, QLR = (2, 256, 256, 192)
        s = lambda k, shape, fan: jax.random.normal(k, shape, jnp.float32) * fan ** (-0.5)
        return {'hidden_states': jax.random.normal(ks[0], (B, S, H), jnp.float32), 'q_a_w': s(ks[1], (QLR, H), H), 'q_a_ln_w': jnp.ones((QLR,), jnp.float32), 'q_b_w': s(ks[2], (NH * D_QK, QLR), QLR), 'kv_a_w': s(ks[3], (KV_LORA + D_ROPE, H), H), 'kv_a_ln_w': jnp.ones((KV_LORA,), jnp.float32), 'kv_b_w': s(ks[4], (NH * (D_NOPE + D_V), KV_LORA), KV_LORA), 'o_w': s(ks[5], (H, NH * D_V), NH * D_V)}
    _L0_attn_in = _L0_attn_setup()

    def _L0_ffn_setup():
        import jax, jax.numpy as jnp
        import numpy as np
        E, D_MODEL, D_FF = (8, 256, 1024)
        B, CAP = (4, 128)
        key = jax.random.key(seed)
        k_x, k_w1, k_w2 = jax.random.split(key, 3)
        scale = 0.02
        x = jax.random.normal(k_x, (B, E * CAP, D_MODEL), dtype=jnp.float32)
        w1 = jax.random.normal(k_w1, (E, D_MODEL, D_FF), dtype=jnp.float32) * scale
        b1 = jnp.zeros((E, D_FF), dtype=jnp.float32)
        w2 = jax.random.normal(k_w2, (E, D_FF, D_MODEL), dtype=jnp.float32) * scale
        b2 = jnp.zeros((E, D_MODEL), dtype=jnp.float32)
        return {'x': x, 'w1': w1, 'b1': b1, 'w2': w2, 'b2': b2}
    _L0_ffn_in = _L0_ffn_setup()
    _d = {'L0_attn_hidden_states': _L0_attn_in['hidden_states'], 'L0_attn_q_a_w': _L0_attn_in['q_a_w'], 'L0_attn_q_a_ln_w': _L0_attn_in['q_a_ln_w'], 'L0_attn_q_b_w': _L0_attn_in['q_b_w'], 'L0_attn_kv_a_w': _L0_attn_in['kv_a_w'], 'L0_attn_kv_a_ln_w': _L0_attn_in['kv_a_ln_w'], 'L0_attn_kv_b_w': _L0_attn_in['kv_b_w'], 'L0_attn_o_w': _L0_attn_in['o_w'], 'L0_ffn_w1': _L0_ffn_in['w1'], 'L0_ffn_b1': _L0_ffn_in['b1'], 'L0_ffn_w2': _L0_ffn_in['w2'], 'L0_ffn_b2': _L0_ffn_in['b2']}
    _x0 = _d['L0_attn_hidden_states']
    _d['L0_attn_hidden_states'] = jax.random.normal(jax.random.fold_in(jax.random.key(seed), 1), (8, 512, 256), dtype=_x0.dtype)
    del _x0
    return _d

def reference(L0_attn_hidden_states, L0_attn_q_a_w, L0_attn_q_a_ln_w, L0_attn_q_b_w, L0_attn_kv_a_w, L0_attn_kv_a_ln_w, L0_attn_kv_b_w, L0_attn_o_w, L0_ffn_w1, L0_ffn_b1, L0_ffn_w2, L0_ffn_b2):

    def _L0_attn_ref(hidden_states, q_a_w, q_a_ln_w, q_b_w, kv_a_w, kv_a_ln_w, kv_b_w, o_w):
        import jax, jax.numpy as jnp
        import numpy as np
        ROPE_THETA = 10000.0
        NH, D_NOPE, D_ROPE, D_V = (16, 128, 64, 128)
        D_QK = D_NOPE + D_ROPE
        KV_LORA = 64
        SCALING = D_QK ** (-0.5)
        EPS = 1e-06

        def rmsnorm(x, w):
            xf = x.astype(jnp.float32)
            var = jnp.mean(xf * xf, axis=-1, keepdims=True)
            return (w * (xf * jax.lax.rsqrt(var + EPS))).astype(x.dtype)

        def rotate_half(x):
            x1, x2 = jnp.split(x, 2, axis=-1)
            return jnp.concatenate([-x2, x1], axis=-1)

        def rope_cos_sin(seq_len, dim, dtype):
            inv_freq = 1.0 / ROPE_THETA ** (jnp.arange(0, dim, 2, dtype=jnp.float32) / dim)
            t = jnp.arange(seq_len, dtype=jnp.float32)
            ang = jnp.outer(t, inv_freq)
            emb = jnp.concatenate([ang, ang], axis=-1)
            return (jnp.cos(emb).astype(dtype), jnp.sin(emb).astype(dtype))
        B, S, H = hidden_states.shape
        q_a = hidden_states @ q_a_w.T
        q = rmsnorm(q_a, q_a_ln_w) @ q_b_w.T
        q = q.reshape(B, S, NH, D_QK).transpose(0, 2, 1, 3)
        q_nope, q_rope = (q[..., :D_NOPE], q[..., D_NOPE:])
        kv_a = hidden_states @ kv_a_w.T
        c_kv, k_rope = (kv_a[..., :KV_LORA], kv_a[..., KV_LORA:])
        kv = rmsnorm(c_kv, kv_a_ln_w) @ kv_b_w.T
        kv = kv.reshape(B, S, NH, D_NOPE + D_V).transpose(0, 2, 1, 3)
        k_nope, v = (kv[..., :D_NOPE], kv[..., D_NOPE:])
        k_rope = k_rope[:, None, :, :]
        cos, sin = rope_cos_sin(S, D_ROPE, hidden_states.dtype)
        q_rope = q_rope * cos + rotate_half(q_rope) * sin
        k_rope = k_rope * cos + rotate_half(k_rope) * sin
        k_rope = jnp.broadcast_to(k_rope, (B, NH, S, D_ROPE))
        q_full = jnp.concatenate([q_nope, q_rope], axis=-1)
        k_full = jnp.concatenate([k_nope, k_rope], axis=-1)
        scores = jnp.einsum('bhqd,bhkd->bhqk', q_full, k_full) * SCALING
        causal = jnp.tril(jnp.ones((S, S), bool))
        scores = jnp.where(causal, scores, jnp.finfo(scores.dtype).min)
        attn = jax.nn.softmax(scores.astype(jnp.float32), axis=-1).astype(v.dtype)
        out = jnp.einsum('bhqk,bhkd->bhqd', attn, v)
        out = out.transpose(0, 2, 1, 3).reshape(B, S, NH * D_V)
        return out @ o_w.T

    def _L0_ffn_ref(x, w1, b1, w2, b2):
        import jax, jax.numpy as jnp
        import numpy as np
        E, D_MODEL, D_FF = (8, 256, 1024)
        B, CAP = (4, 128)
        Bsz, T, d = x.shape
        nE = w1.shape[0]
        cap = T // nE
        xe = x.reshape(Bsz, nE, cap, d)
        h = jnp.einsum('becd,edf->becf', xe, w1) + b1[:, None, :]
        h = jax.nn.gelu(h, approximate=False)
        out = jnp.einsum('becf,efd->becd', h, w2) + b2[:, None, :]
        return out.reshape(Bsz, T, d)
    x = L0_attn_hidden_states
    xn = _layernorm(x, axis=-1)
    s = _L0_attn_ref(xn, L0_attn_q_a_w, L0_attn_q_a_ln_w, L0_attn_q_b_w, L0_attn_kv_a_w, L0_attn_kv_a_ln_w, L0_attn_kv_b_w, L0_attn_o_w)
    g = _silu(_L0_ffn_ref(xn, L0_ffn_w1, L0_ffn_b1, L0_ffn_w2, L0_ffn_b2))
    x = x + s * g
    return x

_drawn_inputs = setup_inputs


def setup_inputs(seed=0):
    import zlib

    import numpy as np

    out = dict(_drawn_inputs(seed))
    spreads = {'L0_attn_q_a_ln_w': (1.0, 0.6),
     'L0_attn_kv_a_ln_w': (1.0, 0.6),
     'L0_ffn_b1': (0.0, 0.8),
     'L0_ffn_b2': (0.0, 0.734)}
    factors = {'L0_attn_q_a_w': 4.016,
     'L0_attn_q_b_w': 4.003,
     'L0_attn_kv_a_w': 3.928,
     'L0_attn_kv_b_w': 3.343,
     'L0_attn_o_w': 3.362,
     'L0_ffn_w1': 4.742,
     'L0_ffn_w2': 4.419}
    for name, (base, spread) in spreads.items():
        noise = np.random.default_rng([zlib.crc32(name.encode()), seed]).standard_normal(out[name].shape)
        drawn = base * np.exp(spread * noise) if base else spread * noise
        out[name] = jnp.asarray(drawn.astype(out[name].dtype))
    for name, factor in factors.items():
        out[name] = (out[name] * factor).astype(out[name].dtype)
    return out
```

```python
from contextlib import ExitStack

import numpy as np

import concourse.bass as bass
from concourse import mybir

FP32 = mybir.dt.float32
FP32R = mybir.dt.float32r
FP16 = mybir.dt.float16
ALU = mybir.AluOpType
ACT = mybir.ActivationFunctionType

P = 128
BATCH, SEQ, DIM = 8, 512, 256
TOKENS = BATCH * SEQ
HEADS, NOPE, ROPE, VDIM = 16, 128, 64, 128
QK = NOPE + ROPE
Q_LORA, KV_LORA = 192, 64
EXPERTS, FF = 8, 1024
CAP = SEQ // EXPERTS
LN_EPS, RMS_EPS = 1e-5, 1e-6
SCALE = QK ** -0.5
ROPE_THETA = 10000.0

TILES = SEQ // P
KD = DIM // P
GROUPS = 4
GH = HEADS // GROUPS
HW = KV_LORA + ROPE
GW = GH * HW
LATENT = Q_LORA + KV_LORA + ROPE
UNITS = HEADS * TILES
FT = FF // P

P_SCALE = 2.0 ** 12
C_SCALE = 2.0 ** 8
NEG = -3.0e38


def fp(ap):
    return ap.bitcast(FP32)


def build(nc, x, q_a_w, q_a_ln, q_b_w, kv_a_w, kv_a_ln, kv_b_w, o_w, w1, b1, w2, b2, cos_t, sin_t, out):
    z_dram = nc.dram_tensor("z_scratch", [TOKENS, DIM], FP32, kind="Internal").ap()
    xt_dram = nc.dram_tensor("xt_scratch", [P, 2, KD, TOKENS], FP32, kind="Internal").ap()
    ctx = ExitStack()
    with ctx:
        def sb(name, shape, dt=FP32, where=ctx):
            return where.enter_context(nc.sbuf_tensor(name, shape, dt))

        bank = [ctx.enter_context(nc.psum_tensor(f"bank{i}", [P, 512], FP32)) for i in range(8)]
        keep = dict(
            ident=sb("ident", [P, P]),
            mask=sb("mask", [P, SEQ]),
            minus_half=sb("minus_half", [P, TILES]),
            cos=sb("cos", [P, TILES, ROPE]),
            sin=sb("sin", [P, TILES, ROPE]),
            wa_h=sb("wa_h", [P, KD, LATENT], FP32R),
            wa_l=sb("wa_l", [P, KD, LATENT], FP32R),
            wq_h=sb("wq_h", [P, 2, HEADS * HW], FP32R),
            wq_l=sb("wq_l", [P, 2, HEADS * HW], FP32R),
            wo_h=sb("wo_h", [P, HEADS // 2, DIM], FP32R),
            wo_l=sb("wo_l", [P, HEADS // 2, DIM], FP32R),
            b1t=sb("b1t", [P, EXPERTS * FT]),
        )
        with ExitStack() as two:
            xt_h = two.enter_context(nc.sbuf_tensor("xt_h", [P, KD, TOKENS], FP32R))
            xt_l = two.enter_context(nc.sbuf_tensor("xt_l", [P, KD, TOKENS], FP32R))
            with ExitStack() as own:
                prepare(nc, own, bank, keep, xt_h, xt_l, xt_dram, x, q_a_w, q_a_ln, q_b_w, kv_a_w, kv_a_ln,
                        kv_b_w, o_w, b1, cos_t, sin_t)
            with ExitStack() as own:
                experts(nc, own, bank, keep, xt_h, xt_l, z_dram, w1, w2, b2)
        with ExitStack() as own:
            attend(nc, own, bank, keep, xt_dram, z_dram, x, out)


def prepare(nc, own, bank, keep, xt_h, xt_l, xt_dram, x, q_a_w, q_a_ln, q_b_w, kv_a_w, kv_a_ln, kv_b_w, o_w,
            b1, cos_t, sin_t):
    def sb(name, shape, dt=FP32):
        return own.enter_context(nc.sbuf_tensor(name, shape, dt))

    def sem(name):
        return own.enter_context(nc.semaphore(name))

    ident, mask, minus_half = keep["ident"], keep["mask"], keep["minus_half"]
    x_in = sb("x_in", [P, 2 * TILES, DIM])
    xn = sb("xn", [P, TILES, DIM])
    stats = sb("stats", [P, TILES, 6])
    mean_var = sb("mean_var", [P, TILES, 2])
    rstd = sb("rstd", [P, TILES])
    wa_in = sb("wa_in", [P, 3, DIM])
    wqn = sb("wqn", [P, HEADS, 2 * P])
    wqr = sb("wqr", [ROPE, HEADS, 2 * P])
    wk = sb("wk", [P, HEADS, KV_LORA])
    wv = sb("wv", [P, HEADS, KV_LORA])
    wo_in = sb("wo_in", [P, KD, HEADS * VDIM])
    wot = sb("wot", [P, 2, 2, DIM])
    b1_in = sb("b1_in", [EXPERTS * FT, P])
    q_ln = sb("q_ln", [P, 2])
    kv_ln = sb("kv_ln", [P, KV_LORA])

    s_x = [sem("x_loaded_even"), sem("x_loaded_odd")]
    s_const = sem("constants_made")
    s_w = sem("weights_loaded")
    s_var = sem("variance_ready")
    s_eps = sem("eps_added")
    s_rstd = sem("rstd_ready")
    s_xn = sem("xn_ready")
    s_tr = sem("transposes_done")
    s_hi = sem("transpose_hi_copied")
    s_lo = sem("transpose_lo_copied")
    s_xt = sem("transposes_stored")
    s_dve = sem("statistics_ready")
    s_passed = sem("waits_passed")
    s_gain = sem("gains_applied")
    s_job = sem("weight_product_done")
    s_job_hi = sem("weight_hi_copied")
    s_job_free = sem("weight_bank_free")

    q_b_rows = q_b_w.rearrange("(h f) r -> f h r", f=QK)
    kv_b_rows = kv_b_w.rearrange("(h f) r -> f h r", f=NOPE + VDIM)

    jobs = [("down", k) for k in range(KD)] + [("bias", 0)]
    jobs += [("query", (g, i)) for g in range(GROUPS) for i in range(2)]
    jobs += [("o_transpose", 0)]
    for j in range(HEADS // 2):
        if j + 1 < HEADS // 2:
            jobs += [("o_transpose", j + 1)]
        jobs += [("output", j)]
    by_scalar = [kind in ("down", "query", "output") for kind, _ in jobs]

    def hi_copies(n):
        return sum(by_scalar[:n])

    with nc.Block() as block:

        @block.sync
        def _(sp):
            with sp.Fori(0, BATCH // 2) as i:
                for odd in range(2):
                    b = 2 * i + odd
                    sp.wait_ge(s_xn, TILES * (b + 1))
                    sp.dma_start(x_in[:, odd * TILES:(odd + 1) * TILES, :],
                                 x[bass.ds(b * SEQ, SEQ), :].rearrange("(t p) d -> p t d", p=P)).then_inc(s_x[odd], 16)

        @block.gpsimd
        def _(pool):
            pool.memset(ident[:], 0.0).then_inc(s_const, 1)
            pool.memset(mask[:], 0.0).then_inc(s_const, 1)
            pool.memset(minus_half[:], -0.5).then_inc(s_const, 1)
            pool.wait_ge(s_const, 3)
            pool.affine_select(out=ident[:], in_=ident[:], compare_op=ALU.not_equal, fill=1.0, base=0,
                               pattern=[[-1, P]], channel_multiplier=1).then_inc(s_const, 1)
            pool.affine_select(out=mask[:, SEQ - P:], in_=mask[:, SEQ - P:], compare_op=ALU.is_ge, fill=NEG,
                               base=0, pattern=[[-1, P]], channel_multiplier=1).then_inc(s_const, 1)
            with pool.Fori(0, BATCH // 2) as i:
                for odd in range(2):
                    b = 2 * i + odd
                    pool.wait_ge(s_var, b + 1)
                    pool.sem_inc(s_passed, 1)
                    pool.tensor_scalar(rstd[:], mean_var[:, :, 1], LN_EPS, None, ALU.add).then_inc(s_eps, 1)
                    pool.wait_ge(s_eps, b + 1)
                    pool.tensor_tensor(rstd[:], rstd[:], minus_half[:, 0:TILES], ALU.pow).then_inc(s_rstd, 1)

        @block.scalar
        def _(act):
            for dst, src in (
                (wa_in[:, 0, :], q_a_w[0:P, :]),
                (wa_in[0:Q_LORA - P, 1, :], q_a_w[P:Q_LORA, :]),
                (wa_in[Q_LORA - P:P, 1, :], kv_a_w[0:KV_LORA, :]),
                (wa_in[0:ROPE, 2, :], kv_a_w[KV_LORA:KV_LORA + ROPE, :]),
                (b1_in[:, :], b1.rearrange("e (k p) -> (e k) p", p=P)),
                (q_ln[:, 0:1], q_a_ln[0:P].unsqueeze(1)),
                (q_ln[0:64, 1:2], q_a_ln[P:Q_LORA].unsqueeze(1)),
                (q_ln[64:P, 1:2], q_a_ln[P:Q_LORA].unsqueeze(1)),
                (kv_ln[:, :], kv_a_ln.unsqueeze(0).to_broadcast([P, KV_LORA])),
                (wqn[:, :, 0:Q_LORA], q_b_rows[0:NOPE]),
                (wqr[:, :, 0:Q_LORA], q_b_rows[NOPE:QK]),
                (wqn[:, :, Q_LORA:], q_b_rows[0:NOPE, :, P:Q_LORA]),
                (wqr[:, :, Q_LORA:], q_b_rows[NOPE:QK, :, P:Q_LORA]),
                (wk[:, :, :], kv_b_rows[0:NOPE]),
                (wv[:, :, :], kv_b_rows[NOPE:NOPE + VDIM]),
                (wo_in[:, :, :], o_w.rearrange("(t p) n -> p t n", p=P)),
                (keep["cos"][:, :, :], cos_t.rearrange("(t p) f -> p t f", p=P)),
                (keep["sin"][:, :, :], sin_t.rearrange("(t p) f -> p t f", p=P)),
            ):
                act.dma_start(dst, src).then_inc(s_w, 16)
            with act.Fori(0, BATCH // 2) as i:
                for odd in range(2):
                    b = 2 * i + odd
                    for k in range(KD):
                        act.wait_ge(s_tr, KD * b + k + 1)
                        act.copy(xt_h[:, k, bass.ds(b * SEQ, SEQ)], bank[k][:, :]).then_inc(s_hi, 1)
                    act.wait_ge(s_lo, KD * (b + 2))
                    act.wait_ge(s_hi, KD * (b + 1))
                    act.dma_start(xt_dram[:, 0, :, bass.ds(b * SEQ, SEQ)], fp(xt_h[:, :, bass.ds(b * SEQ, SEQ)])) \
                        .then_inc(s_xt, 16)
                    act.dma_start(xt_dram[:, 1, :, bass.ds(b * SEQ, SEQ)], fp(xt_l[:, :, bass.ds(b * SEQ, SEQ)])) \
                        .then_inc(s_xt, 16)
            act.wait_ge(s_gain, 2)
            for n, (kind, at) in enumerate(jobs):
                if not by_scalar[n]:
                    continue
                act.wait_ge(s_job, n + 1)
                ps = bank[4 + n % 4]
                if kind == "down":
                    ins = act.copy(keep["wa_h"][:, at, :], ps[:, 0:LATENT])
                elif kind == "query":
                    g, i = at
                    ins = act.activation(keep["wq_h"][:, i, g * GW:(g + 1) * GW], ps[:, :], ACT.Copy,
                                         scale=q_ln[:, i:i + 1])
                else:
                    ins = act.activation(keep["wo_h"][:, at, :], ps[:, 0:DIM], ACT.Copy,
                                         scale=1.0 / (P_SCALE * C_SCALE))
                ins.then_inc(s_job_hi, 1)
            act.wait_ge(s_xt, 32 * BATCH)

        @block.vector
        def _(dve):
            dve.sem_inc(s_xn, 2 * TILES)
            dve.sem_inc(s_lo, KD)
            dve.sem_inc(s_job_free, 4)
            with dve.Fori(0, BATCH // 2) as i:
                for odd in range(2):
                    b = 2 * i + odd
                    dve.wait_ge(s_x[odd], 16 * (i + 1))
                    for t in range(TILES):
                        ins = dve.bn_stats(stats[:, t, :], x_in[:, odd * TILES + t, :])
                    ins.then_inc(s_dve, 1)
                    dve.wait_ge(s_dve, b + 1)
                    dve.sem_inc(s_passed, 1)
                    for t in range(TILES):
                        ins = dve.bn_aggr(mean_var[:, t, :], stats[:, t, :])
                    ins.then_inc(s_var, 1)
                    dve.wait_ge(s_var, b + 1)
                    dve.wait_ge(s_rstd, b + 1)
                    for t in range(TILES):
                        dve.tensor_scalar(xn[:, t, :], x_in[:, odd * TILES + t, :],
                                          mean_var[:, t, 0:1], rstd[:, t:t + 1],
                                          ALU.subtract, ALU.mult).then_inc(s_xn, 1)
                    for k in range(KD):
                        dve.wait_ge(s_hi, KD * b + k + 1)
                        dve.tensor_tensor(xt_l[:, k, bass.ds(b * SEQ, SEQ)], bank[k][:, :],
                                          fp(xt_h[:, k, bass.ds(b * SEQ, SEQ)]), ALU.subtract).then_inc(s_lo, 1)
            dve.wait_ge(s_w, 16 * 18)
            for w in (wk, wv):
                dve.tensor_tensor(w[:, :, :], w[:, :, :],
                                  kv_ln[:, :].unsqueeze(1).to_broadcast([P, HEADS, KV_LORA]),
                                  ALU.mult).then_inc(s_gain, 1)
            for n, (kind, at) in enumerate(jobs):
                if by_scalar[n]:
                    dve.wait_ge(s_job_hi, hi_copies(n) + 1)
                else:
                    dve.wait_ge(s_job, n + 1)
                ps = bank[4 + n % 4]
                if kind == "down":
                    ins = dve.tensor_tensor(keep["wa_l"][:, at, :], ps[:, 0:LATENT], fp(keep["wa_h"][:, at, :]),
                                            ALU.subtract)
                elif kind == "bias":
                    ins = dve.tensor_copy(keep["b1t"][:, :], ps[:, 0:EXPERTS * FT])
                elif kind == "query":
                    g, i = at
                    cols = slice(g * GW, (g + 1) * GW)
                    ins = dve.scalar_tensor_tensor(keep["wq_l"][:, i, cols], ps[:, :], q_ln[:, i:i + 1],
                                                   fp(keep["wq_h"][:, i, cols]), ALU.mult, ALU.subtract)
                elif kind == "o_transpose":
                    ins = dve.tensor_copy(wot[:, at % 2, :, :], ps[:, :].rearrange("p (h n) -> p h n", h=2))
                else:
                    ins = dve.scalar_tensor_tensor(keep["wo_l"][:, at, :], ps[:, 0:DIM], 1.0 / (P_SCALE * C_SCALE),
                                                   fp(keep["wo_h"][:, at, :]), ALU.mult, ALU.subtract)
                ins.then_inc(s_job_free, 1)

        @block.tensor
        def _(pe):
            pe.wait_ge(s_const, 5)
            with pe.Fori(0, BATCH // 2) as i:
                for odd in range(2):
                    b = 2 * i + odd
                    pe.wait_ge(s_xn, 2 * TILES + TILES * (b + 1))
                    for k in range(KD):
                        pe.wait_ge(s_lo, KD * b + k + 1)
                        for t in range(TILES):
                            ins = pe.transpose(bank[k][:, t * P:(t + 1) * P], xn[:, t, k * P:(k + 1) * P], ident[:, :])
                        ins.then_inc(s_tr, 1)
            pe.wait_ge(s_gain, 2)
            for n, (kind, at) in enumerate(jobs):
                pe.wait_ge(s_job_free, n + 1)
                ps = bank[4 + n % 4]
                if kind == "down":
                    for i, rows in enumerate((P, P, ROPE)):
                        ins = pe.transpose(ps[:, i * P:i * P + rows], wa_in[0:rows, i, at * P:(at + 1) * P],
                                           ident[0:rows, 0:rows])
                elif kind == "bias":
                    ins = pe.transpose(ps[:, 0:EXPERTS * FT], b1_in[:, :], ident[0:EXPERTS * FT, 0:EXPERTS * FT])
                elif kind == "query":
                    g, i = at
                    for j in range(GH):
                        h = g * GH + j
                        rows = slice(i * P, (i + 1) * P)
                        pe.matmul(ps[:, j * HW:j * HW + KV_LORA], wqn[:, h, rows], wk[:, h, :], start=True, stop=True)
                        ins = pe.matmul(ps[:, j * HW + KV_LORA:(j + 1) * HW], wqr[:, h, rows], ident[0:ROPE, 0:ROPE],
                                        start=True, stop=True)
                elif kind == "o_transpose":
                    for hh in range(2):
                        for k in range(KD):
                            c = (2 * at + hh) * VDIM
                            ins = pe.transpose(ps[:, hh * DIM + k * P:hh * DIM + (k + 1) * P],
                                               wo_in[:, k, c:c + VDIM], ident[:, :])
                else:
                    pe.wait_ge(s_job_free, 4 + jobs.index(("o_transpose", at)) + 1)
                    for hh in range(2):
                        ins = pe.matmul(ps[hh * 64:hh * 64 + 64, 0:DIM], wv[:, 2 * at + hh, :],
                                        wot[:, at % 2, hh, :], start=True, stop=True)
                ins.then_inc(s_job, 1)


def experts(nc, own, bank, keep, xt_h, xt_l, z_dram, w1, w2, b2):
    def sb(name, shape, dt=FP32):
        return own.enter_context(nc.sbuf_tensor(name, shape, dt))

    def sem(name):
        return own.enter_context(nc.semaphore(name))

    w1_in = sb("w1_in", [P, KD, FF])
    w2_in = sb("w2_in", [P, FT, DIM])
    w1_h, w1_l = sb("w1_h", [P, KD, FF], FP32R), sb("w1_l", [P, KD, FF], FP32R)
    w2_h, w2_l = sb("w2_h", [P, FT, DIM], FP32R), sb("w2_l", [P, FT, DIM], FP32R)
    gelu = sb("gelu", [P, 2, CAP * BATCH])
    act_h = sb("act_h", [P, 4, CAP * BATCH], FP32R)
    act_l = sb("act_l", [P, 4, CAP * BATCH], FP32R)
    z = sb("z", [P, TILES, DIM])
    b2_all = sb("b2_all", [P, EXPERTS, DIM])
    up = bank[0:4]
    down = bank[4:8]
    LAG = 2

    s_w1 = sem("w1_loaded")
    s_w2 = sem("w2_loaded")
    s_b2 = sem("b2_loaded")
    s_w1h = sem("w1_hi_made")
    s_w2h = sem("w2_hi_made")
    s_w1s = sem("w1_split")
    s_w2s = sem("w2_split")
    s_up = sem("up_product_done")
    s_gelu = sem("gelu_done")
    s_act = sem("activation_split")
    s_act_h = sem("activation_hi_made")
    s_down = sem("down_product_step_done")
    s_z = sem("z_ready")
    s_zst = sem("z_stored")

    w1_rows = w1.rearrange("e (k p) f -> p e k f", p=P)
    w2_rows = w2.rearrange("e (k p) n -> p e k n", p=P)
    z_rows = z_dram.rearrange("(q o e c) d -> o c e q d", o=2, e=EXPERTS, c=CAP)

    with nc.Block() as block:

        @block.sync
        def _(sp):
            sp.dma_start(w1_in[:, :, :], w1_rows[:, 0]).then_inc(s_w1, 16)
            sp.dma_start(w2_in[:, :, :], w2_rows[:, 0]).then_inc(s_w2, 16)
            sp.dma_start(b2_all[:, :, :], b2.unsqueeze(0).to_broadcast([P, EXPERTS, DIM])).then_inc(s_b2, 16)
            sp.sem_inc(s_zst, 32)
            with sp.Fori(0, EXPERTS) as e:
                sp.wait_ge(s_w1s, FT * (e + 1))
                sp.dma_start(w1_in[:, :, :], w1_rows[:, bass.ds((e + 1) % EXPERTS, 1)]
                             .rearrange("p e k f -> p (e k) f")).then_inc(s_w1, 16)
                sp.wait_ge(s_w2s, FT * (e + 1))
                sp.dma_start(w2_in[:, :, :], w2_rows[:, bass.ds((e + 1) % EXPERTS, 1)]
                             .rearrange("p e k n -> p (e k) n")).then_inc(s_w2, 16)
                sp.wait_ge(s_z, TILES * (e + 2))
                for o in range(2):
                    sp.dma_start(z_rows[o][:, bass.ds(e, 1)].rearrange("c e q d -> c (e q) d"),
                                 z[o * CAP:(o + 1) * CAP, :, :]).then_inc(s_zst, 16)
            sp.wait_ge(s_w1, 16 * (EXPERTS + 1))
            sp.wait_ge(s_w2, 16 * (EXPERTS + 1))
            sp.wait_ge(s_zst, 32 * (EXPERTS + 1))

        def w1_tile(w, k):
            return w[:, :, k * P:(k + 1) * P]

        @block.scalar
        def _(act):
            def split_w1(loads, k):
                act.wait_ge(s_w1, 16 * loads)
                act.copy(w1_tile(w1_h, k), w1_tile(w1_in, k)).then_inc(s_w1h, 1)

            def split_w2(loads, k):
                act.wait_ge(s_w2, 16 * loads)
                act.copy(w2_h[:, k, :], w2_in[:, k, :]).then_inc(s_w2h, 1)

            act.sem_inc(s_gelu, 4)
            for k in range(FT):
                split_w1(1, k)
            for k in range(FT):
                split_w2(1, k)
            with act.Fori(0, EXPERTS) as e:
                for k in range(FT + LAG + 1):
                    if k < FT:
                        act.wait_ge(s_up, FT * e + k + 1)
                        act.wait_ge(s_act, FT * e + k + 1)
                        act.activation(gelu[:, k % 2, :], up[k % 4][:, :], ACT.Gelu,
                                       bias=keep["b1t"][:, bass.ds(e * FT + k, 1)]).then_inc(s_gelu, 1)
                        split_w1(e + 2, k)
                    if k > LAG:
                        act.wait_ge(s_down, 4 + FT * e + k - LAG)
                        split_w2(e + 2, k - LAG - 1)

        @block.vector
        def _(dve):
            def split_w1(done, k):
                dve.wait_ge(s_w1h, done + k + 1)
                dve.tensor_tensor(w1_tile(w1_l, k), w1_tile(w1_in, k), fp(w1_tile(w1_h, k)),
                                  ALU.subtract).then_inc(s_w1s, 1)

            def split_w2(done, k):
                dve.wait_ge(s_w2h, done + k + 1)
                dve.tensor_tensor(w2_l[:, k, :], w2_in[:, k, :], fp(w2_h[:, k, :]),
                                  ALU.subtract).then_inc(s_w2s, 1)

            dve.sem_inc(s_act, 2)
            dve.sem_inc(s_z, TILES)
            for k in range(FT):
                split_w1(0, k)
            for k in range(FT):
                split_w2(0, k)
            dve.wait_ge(s_b2, 16)
            with dve.Fori(0, EXPERTS) as e:
                for k in range(FT + LAG + 1):
                    if k < FT:
                        dve.wait_ge(s_gelu, 4 + FT * e + k + 1)
                        dve.wait_ge(s_down, FT * e + k + 1)
                        dve.tensor_copy(act_h[:, k % 4, :], gelu[:, k % 2, :]).then_inc(s_act_h, 1)
                        dve.wait_ge(s_act_h, FT * e + k + 1)
                        dve.tensor_tensor(act_l[:, k % 4, :], gelu[:, k % 2, :], fp(act_h[:, k % 4, :]),
                                          ALU.subtract).then_inc(s_act, 1)
                        split_w1(FT * (e + 1), k)
                    if k > LAG:
                        split_w2(FT * (e + 1), k - LAG - 1)
                dve.wait_ge(s_down, 4 + FT * (e + 1))
                dve.wait_ge(s_zst, 32 * (e + 1))
                for t in range(TILES):
                    dve.tensor_tensor(z[:, t:t + 1, :], down[t][:, 0:DIM].unsqueeze(1),
                                      b2_all[:, bass.ds(e, 1), :], ALU.add).then_inc(s_z, 1)

        @block.tensor
        def _(pe):
            pe.sem_inc(s_down, 4)
            x_h = xt_h[:, :, :].rearrange("p k (b s) -> p k b s", s=SEQ)
            x_l = xt_l[:, :, :].rearrange("p k (b s) -> p k b s", s=SEQ)
            with pe.Fori(0, EXPERTS) as e:
                for k in range(FT + LAG):
                    if k < FT:
                        pe.wait_ge(s_w1s, FT * e + k + 1)
                        pe.wait_ge(s_gelu, FT * e + k + 1)
                        ps = up[k % 4][:, :].rearrange("p (b c) -> p b c", c=CAP)
                        n = 0
                        for d in range(KD):
                            for w, xx in ((w1_h, x_h), (w1_l, x_h), (w1_h, x_l)):
                                ins = pe.matmul(ps, w[:, d, k * P:(k + 1) * P], xx[:, d, :, bass.ds(e * CAP, CAP)],
                                                start=(n == 0), stop=(n == 3 * KD - 1))
                                n += 1
                        ins.then_inc(s_up, 1)
                    if k >= LAG:
                        j = k - LAG
                        pe.wait_ge(s_act, 2 + FT * e + j + 1)
                        pe.wait_ge(s_w2s, FT * e + j + 1)
                        if j == 0:
                            pe.wait_ge(s_z, TILES * (e + 1))
                        for t in range(TILES):
                            cols = slice(t * P, (t + 1) * P)
                            n = 0
                            for a, w in ((act_h, w2_h), (act_h, w2_l), (act_l, w2_h)):
                                ins = pe.matmul(down[t][:, 0:DIM], a[:, j % 4, cols], w[:, j, :],
                                                start=(j == 0 and n == 0), stop=(j == FT - 1 and n == 2))
                                n += 1
                        ins.then_inc(s_down, 1)


def attend(nc, own, bank, keep, xt_dram, z_dram, x, out):
    def sb(name, shape, dt=FP32):
        return own.enter_context(nc.sbuf_tensor(name, shape, dt))

    def sem(name):
        return own.enter_context(nc.semaphore(name))

    ident, mask, cos, sin = keep["ident"], keep["mask"], keep["cos"], keep["sin"]

    xs = sb("xs", [P, 2, KD, SEQ], FP32R)
    squares = sb("squares", [P, 2, Q_LORA + KV_LORA])
    mean_sq = sb("mean_sq", [P, 2, 2])
    rms = sb("rms", [P, 2, 2])
    q_lat = sb("q_lat", [P, 2, 2 * P])
    keys = sb("keys", [P, 2, HW])
    turn = sb("turn", [P, 2, 2, ROPE])
    qlt_h = sb("qlt_h", [P, 2, SEQ], FP32R)
    qlt_l = sb("qlt_l", [P, SEQ], FP32R)
    keyt_h = sb("keyt_h", [P, 2, SEQ], FP32R)
    keyt_l = sb("keyt_l", [P, 2, SEQ], FP32R)
    lat = sb("lat", [P, 2 * TILES, 2, KV_LORA], FP16)
    q_tok = sb("q_tok", [P, TILES, GH, HW])
    q_turn = sb("q_turn", [P, 2, GH, ROPE])
    qt_h = sb("qt_h", [P, 2, GH, SEQ], FP32R)
    qt_l = sb("qt_l", [P, 2, GH, SEQ], FP32R)
    scores = sb("scores", [P, 2, SEQ])
    neg_max = sb("neg_max", [P, 2])
    probs = sb("probs", [P, 4, SEQ])
    sums = sb("sums", [P, 2, TILES])
    inv_sums = sb("inv_sums", [P, 2, TILES])
    pt_h = sb("pt_h", [P, 4, TILES, P], FP16)
    pt_l = sb("pt_l", [P, 4, TILES, P], FP16)
    mixed2 = sb("mixed2", [P, 2, TILES, 2, KV_LORA])
    mixed = sb("mixed", [P, TILES, HEADS * KV_LORA])
    mt_h = sb("mt_h", [P, 2, HEADS // 2, P], FP32R)
    mt_l = sb("mt_l", [P, 2, HEADS // 2, P], FP32R)
    x_res = sb("x_res", [P, TILES, DIM])
    gate = sb("gate", [P, TILES, DIM])
    tanh = sb("tanh", [P, TILES, DIM])
    result = sb("result", [P, TILES, DIM])

    score_bank, turned_bank, mix_bank, work_bank = bank[0:2], bank[2:4], bank[4:6], bank[6:8]

    s_xs = sem("tokens_loaded")
    s_res = sem("residual_and_gate_loaded")
    s_tanh = sem("tanh_ready")
    s_result = sem("result_ready")
    s_stored = sem("result_stored")
    s_scores = sem("score_bank_ready")
    s_scores_free = sem("score_bank_free")
    s_probs = sem("probs_ready")
    s_turned = sem("probs_transposed")
    s_pt_h = sem("probs_hi_copied")
    s_pt = sem("probs_split")
    s_mix = sem("mix_step_done")
    s_inv = sem("inverse_sums_ready")
    s_mix_free = sem("mix_bank_free")
    s_mixed = sem("head_mixed")
    s_work = sem("work_bank_ready")
    s_work_hi = sem("work_bank_copied_by_scalar")
    s_work_free = sem("work_bank_free")
    s_eps = sem("rms_eps_added")
    s_rms = sem("rms_ready")
    s_keys = sem("latents_normed")
    s_split = sem("latents_hi_made")
    s_qturn = sem("query_rotation_products_ready")
    s_qtok = sem("queries_turned")
    s_passed = sem("waits_passed")

    NEXT = [("latent", 0), ("latent", 1), ("flip", 0), ("latent", 2), ("flip", 1), ("latent", 3), ("flip", 2),
            ("flip", 3)] + [("query", (0, t)) for t in range(TILES)] + [("queryT", (0, j)) for j in range(GH)]
    beside = {}
    n = 0
    for g in range(GROUPS):
        if g + 1 < GROUPS:
            todo = [("query", (g + 1, t)) for t in range(TILES)] + [("queryT", (g + 1, j)) for j in range(GH)]
            steps = range(1, 16, 2)
        else:
            todo, steps = NEXT, range(16)
        for step, job in zip(steps, todo):
            beside[16 * g + step] = (n, *job)
            n += 1
    OUT_JOBS = n
    JOBS = OUT_JOBS + 2 * TILES
    FIRST = len(NEXT)
    LAG_T, LAG_M = 3, 5
    STEPS = UNITS + LAG_M + 1
    BANKS = UNITS + TILES
    assert JOBS % 2 == 0 and FIRST % 2 == 0 and BANKS % 2 == 0

    by_vector = [job != "query" for _, job, _ in sorted(beside.values())] + [True] * (2 * TILES)
    FIRST_FREED, FREED = sum(kind != "query" for kind, _ in NEXT), sum(by_vector)

    def freed_first(n):
        return sum(kind != "query" for kind, _ in NEXT[:n])

    def freed(b, n):
        return FIRST_FREED + FREED * b + sum(by_vector[:n])

    def queries_freed(b, g, j):
        if g == 0:
            return FIRST_FREED + FREED * b - GH + j + 1
        return freed(b, 1 + next(n for n, kind, at in beside.values() if (kind, at) == ("queryT", (g, j))))

    def keys_of(u):
        return (u % TILES + 1) * P

    with nc.Block() as block:

        @block.sync
        def _(sp):
            sp.sem_inc(s_stored, 16)
            for part in range(2):
                sp.dma_start(fp(xs[:, part, :, :]), xt_dram[:, part, :, 0:SEQ]).then_inc(s_xs, 16)
            with sp.Fori(0, BATCH) as b:
                rows = bass.ds(b * SEQ, SEQ)
                sp.wait_ge(s_result, TILES * (b + 1))
                sp.dma_start(x_res[:, :, :], x[rows, :].rearrange("(t p) d -> p t d", p=P)).then_inc(s_res, 16)
                sp.dma_start(gate[:, :, :], z_dram[rows, :].rearrange("(t p) d -> p t d", p=P)).then_inc(s_res, 16)
                sp.wait_ge(s_work, JOBS * b + NEXT.index(("latent", TILES - 1)) + 1)
                for part in range(2):
                    sp.dma_start(fp(xs[:, part, :, :]), xt_dram[:, part, :, bass.ds((b + 1) % BATCH * SEQ, SEQ)]) \
                        .then_inc(s_xs, 16)
                sp.wait_ge(s_result, TILES * (b + 2))
                sp.dma_start(out[rows, :].rearrange("(t p) d -> p t d", p=P), result[:, :, :]).then_inc(s_stored, 16)
            sp.wait_ge(s_xs, 32 * (BATCH + 1))
            sp.wait_ge(s_stored, 16 * (BATCH + 1))

        @block.gpsimd
        def _(pool):
            def latent(job, done, t):
                pool.wait_ge(s_work_hi, job + 1)
                pool.sem_inc(s_passed, 1)
                pool.tensor_scalar(rms[:, t % 2, :], mean_sq[:, t % 2, :], RMS_EPS, None, ALU.add).then_inc(s_eps, 1)
                pool.wait_ge(s_eps, done + t + 1)
                pool.tensor_tensor(rms[:, t % 2, :], rms[:, t % 2, :], keep["minus_half"][:, 0:2],
                                   ALU.pow).then_inc(s_rms, 1)

            def query(job, done, t):
                pool.wait_ge(s_work_hi, job + 1)
                pool.wait_ge(s_qtok, done + t + 1)
                src = q_tok[:, t, :, KV_LORA:]
                pool.tensor_tensor(q_turn[:, 0], src, cos[:, t, :].unsqueeze(1).to_broadcast([P, GH, ROPE]),
                                   ALU.mult)
                pool.tensor_tensor(q_turn[:, 1].rearrange("p h (a f) -> p h a f", a=2),
                                   src.rearrange("p h (a f) -> p h a f", a=2)[:, :, ::-1, :],
                                   sin[:, t, :].rearrange("p (a f) -> p a f", a=2).unsqueeze(1)
                                   .to_broadcast([P, GH, 2, ROPE // 2]), ALU.mult).then_inc(s_qturn, 1)
                pool.wait_ge(s_qturn, done + t + 1)
                pool.tensor_tensor(src, q_turn[:, 0], q_turn[:, 1], ALU.add).then_inc(s_qtok, 1)

            pool.sem_inc(s_qtok, 1)
            pool.sem_inc(s_mixed, 2)
            for n, (kind, at) in enumerate(NEXT):
                if kind == "latent":
                    latent(n, 0, at)
                elif kind == "query":
                    query(n, 0, at[1])
            with pool.Fori(0, BATCH) as b:
                for s in range(STEPS):
                    if s in beside:
                        n, kind, at = beside[s]
                        if kind == "latent":
                            latent(FIRST + JOBS * b + n, TILES * (b + 1), at)
                        elif kind == "query":
                            query(FIRST + JOBS * b + n, TILES * GROUPS * b + TILES * (s // 16 + 1), at[1])
                    if s % TILES == 1 and s >= 9:
                        h = (s - 9) // TILES
                        pool.wait_ge(s_mix_free, 2 + HEADS * b + h + 1)
                        pool.tensor_tensor(mixed[:, :, h * KV_LORA:(h + 1) * KV_LORA], mixed2[:, h % 2, :, 0, :],
                                           mixed2[:, h % 2, :, 1, :], ALU.add).then_inc(s_mixed, 1)

        @block.scalar
        def _(act):
            def take(index, n, kind, at, par):
                act.wait_ge(s_work, index + 1)
                ps = work_bank[n % 2]
                if kind == "latent":
                    act.activation(squares[:, at % 2, 0:Q_LORA], ps[:, 0:Q_LORA], ACT.Square,
                                   scale=float(Q_LORA) ** -0.5, accum_out=mean_sq[:, at % 2, 0:1])
                    ins = act.activation(squares[:, at % 2, Q_LORA:], ps[:, Q_LORA:Q_LORA + KV_LORA], ACT.Square,
                                         scale=float(KV_LORA) ** -0.5, accum_out=mean_sq[:, at % 2, 1:2])
                elif kind == "flip":
                    cols = slice(at * P, (at + 1) * P)
                    act.copy(qlt_h[:, :, cols], ps[:, 0:2 * P].rearrange("p (a c) -> p a c", a=2))
                    ins = act.copy(keyt_h[:, bass.ds(par, 1), cols], ps[:, 2 * P:3 * P].unsqueeze(1))
                elif kind == "query":
                    g, t = at
                    ins = act.copy(q_tok[:, t, :, :], ps[:, :].rearrange("p (h f) -> p h f", h=GH))
                elif kind == "queryT":
                    g, j = at
                    ins = act.copy(qt_h[:, g % 2, j, :], ps[:, :])
                else:
                    t, half = at
                    ins = act.copy(mt_h[:, t % 2, 4 * half:4 * half + 4, :],
                                   ps[:, :].rearrange("p (j c) -> p j c", c=P))
                ins.then_inc(s_work_hi, 1)

            act.sem_inc(s_probs, 2)
            for n, (kind, at) in enumerate(NEXT):
                take(n, n, kind, at, 0)
            with act.Fori(0, BATCH) as b:
                for s in range(STEPS):
                    u = s - LAG_T
                    if 0 <= u < UNITS:
                        act.wait_ge(s_turned, 4 + UNITS * b + u + 1)
                        act.wait_ge(s_mix, UNITS * b + u + 1)
                        m = u % TILES + 1
                        act.activation(pt_h[:, u % 4, 0:m, :],
                                       turned_bank[u % 2][:, 0:m * P].rearrange("p (m c) -> p m c", c=P),
                                       ACT.Copy, scale=P_SCALE).then_inc(s_pt_h, 1)
                    if s < UNITS:
                        act.wait_ge(s_scores_free, 2 + BANKS * b + s + 1)
                        act.wait_ge(s_turned, UNITS * b + s + 1)
                        act.activation(probs[:, s % 4, 0:keys_of(s)], scores[:, s % 2, 0:keys_of(s)], ACT.Exp,
                                       scale=-1.0, bias=neg_max[:, s % 2:s % 2 + 1],
                                       accum_out=sums[:, s // TILES % 2, s % TILES:s % TILES + 1]) \
                            .then_inc(s_probs, 1)
                    if s in beside:
                        n, kind, at = beside[s]
                        take(FIRST + JOBS * b + n, n, kind, at, (b + 1) % 2)
                    if s == 20:
                        act.wait_ge(s_res, 32 * (b + 1))
                        act.activation(tanh[:, :, :], gate[:, :, :], ACT.Tanh, scale=0.5).then_inc(s_tanh, 1)
                for t in range(TILES):
                    for half in range(2):
                        n = OUT_JOBS + 2 * t + half
                        take(FIRST + JOBS * b + n, n, "mixedT", (t, half), None)

        @block.vector
        def _(dve):
            def take(index, back, n, kind, at, par, lat_done):
                ps = work_bank[n % 2]
                if kind == "latent":
                    t = at
                    dve.wait_ge(s_rms, lat_done + t + 1)
                    dve.wait_ge(s_split, lat_done + t + 1)
                    dve.tensor_scalar(q_lat[:, t % 2, 0:Q_LORA], ps[:, 0:Q_LORA], rms[:, t % 2, 0:1], None, ALU.mult)
                    dve.tensor_scalar(q_lat[:, t % 2, Q_LORA:], ps[:, P:Q_LORA], rms[:, t % 2, 0:1], None, ALU.mult)
                    dve.tensor_scalar(keys[:, t % 2, 0:KV_LORA], ps[:, Q_LORA:Q_LORA + KV_LORA],
                                      rms[:, t % 2, 1:2], None, ALU.mult)
                    src = ps[:, Q_LORA + KV_LORA:LATENT]
                    dve.tensor_tensor(turn[:, t % 2, 0, :], src, cos[:, t, :], ALU.mult)
                    dve.tensor_tensor(turn[:, t % 2, 1, :].rearrange("p (a f) -> p a f", a=2),
                                      src.rearrange("p (a f) -> p a f", a=2)[:, ::-1, :],
                                      sin[:, t, :].rearrange("p (a f) -> p a f", a=2),
                                      ALU.mult).then_inc(s_work_free, 1)
                    dve.wait_ge(s_work_free, back)
                    dve.tensor_tensor(keys[:, t % 2, KV_LORA:], turn[:, t % 2, 0, :], turn[:, t % 2, 1, :],
                                      ALU.add).then_inc(s_keys, 1)
                    row = bass.ds(par * TILES + t, 1)
                    src = keys[:, t % 2, 0:KV_LORA].unsqueeze(1)
                    dve.tensor_scalar(lat[:, row, 0, :], src, C_SCALE, None, ALU.mult).then_inc(s_split, 1)
                    dve.wait_ge(s_split, 1 + lat_done + t + 1)
                    dve.scalar_tensor_tensor(lat[:, row, 1, :], src, C_SCALE, lat[:, row, 0, :], ALU.mult,
                                             ALU.subtract)
                    return
                dve.wait_ge(s_work_hi, index + 1)
                if kind == "flip":
                    cols = slice(at * P, (at + 1) * P)
                    dve.tensor_tensor(qlt_l[:, cols], ps[:, 0:P], fp(qlt_h[:, 0, cols]), ALU.subtract)
                    dve.tensor_tensor(qlt_h[64:P, 1, cols], ps[64:P, P:2 * P], fp(qlt_h[64:P, 1, cols]),
                                      ALU.subtract)
                    ins = dve.tensor_tensor(keyt_l[:, bass.ds(par, 1), cols], ps[:, 2 * P:3 * P].unsqueeze(1),
                                            fp(keyt_h[:, bass.ds(par, 1), cols]), ALU.subtract)
                elif kind == "queryT":
                    g, j = at
                    ins = dve.tensor_tensor(qt_l[:, g % 2, j, :], ps[:, :], fp(qt_h[:, g % 2, j, :]), ALU.subtract)
                else:
                    t, half = at
                    part = slice(4 * half, 4 * half + 4)
                    ins = dve.tensor_tensor(mt_l[:, t % 2, part, :], ps[:, :].rearrange("p (j c) -> p j c", c=P),
                                            fp(mt_h[:, t % 2, part, :]), ALU.subtract)
                ins.then_inc(s_work_free, 1)

            for free, count in ((s_scores_free, 2), (s_pt, 2), (s_mix_free, 2), (s_result, TILES), (s_split, 1)):
                dve.sem_inc(free, count)
            for n, (kind, at) in enumerate(NEXT):
                if kind != "query":
                    take(n, freed_first(n + 1), n, kind, at, 0, 0)
            with dve.Fori(0, BATCH) as b:
                def beside_step(s):
                    if s in beside and beside[s][1] != "query":
                        n, kind, at = beside[s]
                        take(FIRST + JOBS * b + n, freed(b, n + 1), n, kind, at, (b + 1) % 2, TILES * (b + 1))

                for s in range(STEPS):
                    if s < UNITS:
                        N = keys_of(s)
                        dve.wait_ge(s_scores, BANKS * b + s + 1)
                        dve.wait_ge(s_probs, UNITS * b + s + 1)
                        dve.sem_inc(s_passed, 1)
                        dve.tensor_tensor_reduce(out=scores[:, s % 2, 0:N], in0=score_bank[s % 2][:, 0:N],
                                                 in1=mask[:, SEQ - N:SEQ], scale=-SCALE, scalar=-NEG,
                                                 op0=ALU.add, op1=ALU.min,
                                                 accum_out=neg_max[:, s % 2:s % 2 + 1])\
                            .then_inc(s_scores_free, 1)
                    beside_step(s - 1)
                    u = s - LAG_T
                    if 0 <= u < UNITS:
                        m = u % TILES + 1
                        dve.wait_ge(s_pt_h, UNITS * b + u + 1)
                        dve.scalar_tensor_tensor(pt_l[:, u % 4, 0:m, :],
                                                 turned_bank[u % 2][:, 0:m * P].rearrange("p (m c) -> p m c", c=P),
                                                 P_SCALE, pt_h[:, u % 4, 0:m, :], ALU.mult,
                                                 ALU.subtract).then_inc(s_pt, 1)
                    if s % TILES == 2 and 6 <= s < UNITS + 4:
                        h = (s - 6) // TILES
                        dve.wait_ge(s_probs, 2 + UNITS * b + TILES * (h + 1))
                        dve.reciprocal(inv_sums[:, h % 2, :], sums[:, h % 2, :]).then_inc(s_inv, 1)
                    if s % TILES == 1 and s >= 9:
                        h = (s - 9) // TILES
                        dve.wait_ge(s_mix, 4 + UNITS * b + TILES * (h + 1))
                        dve.wait_ge(s_inv, HEADS * b + h + 1)
                        dve.wait_ge(s_mixed, HEADS * b + h + 1)
                        dve.tensor_tensor(mixed2[:, h % 2], mix_bank[h % 2][:, :]
                                          .rearrange("p (t a c) -> p t a c", a=2, c=KV_LORA),
                                          inv_sums[:, h % 2, :].unsqueeze(2).unsqueeze(3)
                                          .to_broadcast([P, TILES, 2, KV_LORA]), ALU.mult).then_inc(s_mix_free, 1)
                    if s == 24:
                        dve.wait_ge(s_tanh, b + 1)
                        dve.scalar_tensor_tensor(gate[:, :, :], tanh[:, :, :], 1.0, gate[:, :, :], ALU.add, ALU.mult)

                def output(t):
                    dve.wait_ge(s_scores, BANKS * b + UNITS + t + 1)
                    if t == 0:
                        dve.wait_ge(s_stored, 16 * (b + 1))
                    dve.tensor_tensor(result[:, t, :], score_bank[t % 2][:, 0:DIM], gate[:, t, :],
                                      ALU.mult).then_inc(s_scores_free, 1)
                    dve.wait_ge(s_scores_free, 2 + BANKS * b + UNITS + t + 1)
                    dve.scalar_tensor_tensor(result[:, t, :], result[:, t, :], 0.5, x_res[:, t, :], ALU.mult,
                                             ALU.add).then_inc(s_result, 1)

                for t in range(TILES):
                    for half in range(2):
                        n = OUT_JOBS + 2 * t + half
                        take(FIRST + JOBS * b + n, freed(b, n + 1), n, "mixedT", (t, half), None, None)
                    if t >= 1:
                        output(t - 1)
                output(TILES - 1)

        @block.tensor
        def _(pe):
            def three(ps, parts):
                n = 0
                for (a_h, a_l), (w_h, w_l) in parts:
                    for a, w in ((a_h, w_h), (a_h, w_l), (a_l, w_h)):
                        ins = pe.matmul(ps, a, w, start=(n == 0), stop=(n == 3 * len(parts) - 1))
                        n += 1
                return ins

            def make(index, bank_free, n, kind, at, lat_done, q_done):
                if bank_free is not None:
                    pe.wait_ge(*bank_free)
                ps = work_bank[n % 2]
                if kind == "latent":
                    if at == 0:
                        pe.wait_ge(s_xs, 32 * (lat_done + 1))
                    cols = slice(at * P, (at + 1) * P)
                    ins = three(ps[:, 0:LATENT],
                                [((xs[:, 0, k, cols], xs[:, 1, k, cols]), (keep["wa_h"][:, k, :], keep["wa_l"][:, k, :]))
                                 for k in range(KD)])
                elif kind == "flip":
                    pe.wait_ge(s_keys, lat_done * TILES + at + 1)
                    pe.transpose(ps[:, 0:P], q_lat[:, at % 2, 0:P], ident[:, :])
                    pe.transpose(ps[:, P:2 * P], q_lat[:, at % 2, P:], ident[:, :])
                    ins = pe.transpose(ps[:, 2 * P:3 * P], keys[:, at % 2, :], ident[:, :])
                elif kind == "query":
                    g, t = at
                    rows, cols = slice(t * P, (t + 1) * P), slice(g * GW, (g + 1) * GW)
                    wq_h, wq_l = keep["wq_h"], keep["wq_l"]
                    pairs = ((qlt_h[:, 0, rows], wq_h[:, 0, cols]), (qlt_h[:, 0, rows], wq_l[:, 0, cols]),
                             (qlt_l[:, rows], wq_h[:, 0, cols]),
                             (qlt_h[:, 1, rows], wq_h[:, 1, cols]), (qlt_h[:, 1, rows], wq_l[:, 1, cols]))
                    for i, (a, w) in enumerate(pairs):
                        ins = pe.matmul(ps[:, :], a, w, start=(i == 0), stop=(i == len(pairs) - 1))
                elif kind == "queryT":
                    g, j = at
                    if j == 0:
                        pe.wait_ge(s_qtok, 1 + q_done + TILES)
                    for t in range(TILES):
                        ins = pe.transpose(ps[:, t * P:(t + 1) * P], q_tok[:, t, j, :], ident[:, :])
                else:
                    t, half = at
                    for j in range(4):
                        c = (4 * half + j) * P
                        ins = pe.transpose(ps[:, j * P:(j + 1) * P], mixed[:, t, c:c + P], ident[:, :])
                ins.then_inc(s_work, 1)

            pe.sem_inc(s_turned, 4)
            pe.sem_inc(s_mix, 4)
            for n, (kind, at) in enumerate(NEXT):
                bank_free = None
                if n >= 2:
                    bank_free = (s_work_hi, n - 1) if NEXT[n - 2][0] == "query" else (s_work_free, freed_first(n - 1))
                make(n, bank_free, n, kind, at, 0, 0)
            with pe.Fori(0, BATCH) as b:
                def bank_free(n):
                    if n >= 2 and not by_vector[n - 2]:
                        return s_work_hi, FIRST + JOBS * b + n - 1
                    return s_work_free, freed(b, n - 1) if n >= 1 else freed(b, 0) - 1

                for s in range(STEPS):
                    if s < UNITS:
                        h, t = s // TILES, s % TILES
                        g, j = h // GH, h % GH
                        if t == 0:
                            pe.wait_ge(s_work_free, queries_freed(b, g, j))
                        pe.wait_ge(s_scores_free, BANKS * b + s + 1)
                        N = max(keys_of(s), 2 * P)
                        rows = slice(t * P, (t + 1) * P)
                        par = bass.ds(b % 2, 1)
                        ps = score_bank[s % 2][:, 0:N].unsqueeze(1)
                        three(ps, [((qt_h[:, g % 2, j, rows], qt_l[:, g % 2, j, rows]),
                                          (keyt_h[:, par, 0:N], keyt_l[:, par, 0:N]))]).then_inc(s_scores, 1)
                    u = s - LAG_T
                    if 0 <= u < UNITS:
                        pe.wait_ge(s_probs, 2 + UNITS * b + u + 1)
                        pe.wait_ge(s_pt, UNITS * b + u + 1)
                        for k in range(u % TILES + 1):
                            ins = pe.transpose(turned_bank[u % 2][:, k * P:(k + 1) * P],
                                               probs[:, u % 4, k * P:(k + 1) * P], ident[:, :])
                        ins.then_inc(s_turned, 1)
                    u = s - LAG_M
                    if 0 <= u < UNITS:
                        h, t = u // TILES, u % TILES
                        pe.wait_ge(s_pt, 2 + UNITS * b + u + 1)
                        if t == 0:
                            pe.wait_ge(s_mix_free, HEADS * b + h + 1)
                        for k in range(t + 1):
                            for i, pt in enumerate((pt_h, pt_l)):
                                ins = pe.matmul(mix_bank[h % 2][:, t * P:(t + 1) * P].unsqueeze(1), pt[:, u % 4, k, :],
                                                lat[:, bass.ds(b % 2 * TILES + k, 1), :, :]
                                                .rearrange("p o a c -> p o (a c)"),
                                                start=(k == 0 and i == 0), stop=(k == t and i == 1))
                        ins.then_inc(s_mix, 1)
                    if s in beside:
                        n, kind, at = beside[s]
                        make(FIRST + JOBS * b + n, bank_free(n), n, kind, at, b + 1, TILES * GROUPS * b + TILES * (s // 16 + 1))
                pe.wait_ge(s_mixed, 2 + HEADS * (b + 1))

                def project(t):
                    pe.wait_ge(s_work_free, freed(b, OUT_JOBS + 2 * t + 2))
                    pe.wait_ge(s_scores_free, BANKS * b + UNITS + t + 1)
                    three(score_bank[t % 2][:, 0:DIM],
                          [((mt_h[:, t % 2, j, :], mt_l[:, t % 2, j, :]), (keep["wo_h"][:, j, :], keep["wo_l"][:, j, :]))
                           for j in range(HEADS // 2)]).then_inc(s_scores, 1)

                for t in range(TILES):
                    for half in range(2):
                        n = OUT_JOBS + 2 * t + half
                        make(FIRST + JOBS * b + n, bank_free(n), n, "mixedT", (t, half), None, None)
                    if t >= 1:
                        project(t - 1)
                project(TILES - 1)


_INS = ["L0_attn_hidden_states", "L0_attn_q_a_w", "L0_attn_q_a_ln_w", "L0_attn_q_b_w", "L0_attn_kv_a_w",
        "L0_attn_kv_a_ln_w", "L0_attn_kv_b_w", "L0_attn_o_w", "L0_ffn_w1", "L0_ffn_b1", "L0_ffn_w2", "L0_ffn_b2"]


def rope_tables():
    f32 = np.float32
    inv_freq = f32(1.0) / f32(ROPE_THETA) ** (np.arange(0, ROPE, 2, dtype=f32) / f32(ROPE))
    angle = np.outer(np.arange(SEQ, dtype=f32), inv_freq.astype(f32)).astype(f32)
    cos, sin = np.cos(angle), np.sin(angle)
    return (np.concatenate([cos, cos], axis=-1).astype(f32), np.concatenate([-sin, sin], axis=-1).astype(f32))


def kernel(**inputs):
    import concourse.bacc as bacc
    from concourse.bass_utils import run_bass_kernel_spmd

    nc = bacc.Bacc("TRN2", target_bir_lowering=False, num_devices=1)
    arrays = {name: np.ascontiguousarray(inputs[name]) for name in _INS}
    arrays["L0_attn_hidden_states"] = arrays["L0_attn_hidden_states"].reshape(TOKENS, DIM)
    arrays["cos_table"], arrays["sin_table"] = rope_tables()
    args = [nc.dram_tensor(f"in_{n}", a.shape, mybir.dt.from_np(a.dtype), kind="ExternalInput").ap()
            for n, a in arrays.items()]
    out = nc.dram_tensor("out", (TOKENS, DIM), FP32, kind="ExternalOutput").ap()
    build(nc, *args, out)
    r = run_bass_kernel_spmd(nc, [{f"in_{n}": a for n, a in arrays.items()}], core_ids=[0])
    return r.results[0]["out"].reshape(BATCH, SEQ, DIM)
```

```python
from contextlib import ExitStack

import numpy as np

import concourse.bass as bass
from concourse import mybir

FP32 = mybir.dt.float32
FP32R = mybir.dt.float32r
FP16 = mybir.dt.float16
ALU = mybir.AluOpType
ACT = mybir.ActivationFunctionType

P = 128
BATCH, SEQ, DIM = 8, 512, 256
TOKENS = BATCH * SEQ
HEADS, NOPE, ROPE, VDIM = 16, 128, 64, 128
QK = NOPE + ROPE
Q_LORA, KV_LORA = 192, 64
EXPERTS, FF = 8, 1024
CAP = SEQ // EXPERTS
LN_EPS, RMS_EPS = 1e-5, 1e-6
SCALE = QK ** -0.5
ROPE_THETA = 10000.0

TILES = SEQ // P
KD = DIM // P
GROUPS = 4
GH = HEADS // GROUPS
HW = KV_LORA + ROPE
GW = GH * HW
LATENT = Q_LORA + KV_LORA + ROPE
PAIRS = HEADS // 2
UNITS = HEADS * TILES
FT = FF // P

QUERY_STEPS = ((0, 2, 4, 6), (17, 19, 21, 23), (35, 37, 39, 41))
QUERY_TURN_STEPS = ((10, 12, 14, 16), (26, 30, 32, 34), (46, 49, 50, 51))
LATENT_DELAY = 3
MIXED_TURN_STEPS = (20, 28, 36, 44, 55, 61, 66)
NEXT_STEPS = ((25, ("latent", 0)), (29, ("latent", 1)), (42, ("flip", 0)), (43, ("latent", 2)), (47, ("flip", 1)),
              (52, ("flip", 2)), (53, ("latent", 3)), (54, ("query", (0, 0))), (56, ("flip", 3)),
              (57, ("query", (0, 1))), (59, ("query", (0, 2))), (60, ("query", (0, 3))),
              (63, ("queryT", (0, 0))), (64, ("queryT", (0, 1))), (65, ("queryT", (0, 2))), (67, ("queryT", (0, 3))))

P_SCALE = 2.0 ** 12
C_SCALE = 2.0 ** 8
NEG = -3.0e38


def fp(ap):
    return ap.bitcast(FP32)


def build(nc, x, q_a_w, q_a_ln, q_b_w, kv_a_w, kv_a_ln, kv_b_w, o_w, w1, b1, w2, b2, cos_t, sin_t, out):
    z_dram = nc.dram_tensor("z_scratch", [TOKENS, DIM], FP32, kind="Internal").ap()
    xt_dram = nc.dram_tensor("xt_scratch", [P, 2, KD, TOKENS], FP32, kind="Internal").ap()
    ctx = ExitStack()
    with ctx:
        def sb(name, shape, dt=FP32, where=ctx):
            return where.enter_context(nc.sbuf_tensor(name, shape, dt))

        bank = [ctx.enter_context(nc.psum_tensor(f"bank{i}", [P, 512], FP32)) for i in range(8)]
        keep = dict(
            ident=sb("ident", [P, P]),
            mask=sb("mask", [P, SEQ]),
            minus_half=sb("minus_half", [P, TILES]),
            wa_h=sb("wa_h", [P, KD, LATENT], FP32R),
            wa_l=sb("wa_l", [P, KD, LATENT], FP32R),
            wq_h=sb("wq_h", [P, 2, HEADS * HW], FP32R),
            wq_l=sb("wq_l", [P, 2, HEADS * HW], FP32R),
            wo_h=sb("wo_h", [P, HEADS // 2, DIM], FP32R),
            wo_l=sb("wo_l", [P, HEADS // 2, DIM], FP32R),
            b1t=sb("b1t", [P, EXPERTS * FT]),
        )
        with ExitStack() as two:
            xt_h = two.enter_context(nc.sbuf_tensor("xt_h", [P, KD, TOKENS], FP32R))
            xt_l = two.enter_context(nc.sbuf_tensor("xt_l", [P, KD, TOKENS], FP32R))
            pre = dict(
                w1_in=sb("w1_in", [P, 2, KD, FF], where=two),
                w2_in=sb("w2_in", [P, FT, DIM], where=two),
                b2_all=sb("b2_all", [P, EXPERTS, DIM], where=two),
                s_w1=two.enter_context(nc.semaphore("w1_loaded")),
                s_w2=two.enter_context(nc.semaphore("w2_loaded")),
                s_b2=two.enter_context(nc.semaphore("b2_loaded")),
            )
            with ExitStack() as own:
                prepare(nc, own, bank, keep, pre, xt_h, xt_l, x, q_a_w, q_a_ln, q_b_w, kv_a_w, kv_a_ln, kv_b_w, o_w,
                        b1, w1, w2, b2)
            with ExitStack() as own:
                experts(nc, own, bank, keep, pre, xt_h, xt_l, xt_dram, z_dram, w1, w2)
        with ExitStack() as own:
            attend(nc, own, bank, keep, xt_dram, z_dram, x, cos_t, sin_t, out)


def prepare(nc, own, bank, keep, pre, xt_h, xt_l, x, q_a_w, q_a_ln, q_b_w, kv_a_w, kv_a_ln, kv_b_w, o_w, b1, w1,
            w2, b2):
    assert BATCH == PAIRS

    def sb(name, shape, dt=FP32):
        return own.enter_context(nc.sbuf_tensor(name, shape, dt))

    def sem(name):
        return own.enter_context(nc.semaphore(name))

    ident, mask, minus_half = keep["ident"], keep["mask"], keep["minus_half"]
    x_in = sb("x_in", [P, 2, TILES, DIM])
    xn = sb("xn", [P, TILES, DIM])
    stats = sb("stats", [P, TILES, 6])
    mean_var = sb("mean_var", [P, TILES, 2])
    rstd = sb("rstd", [P, TILES])
    wa_in = sb("wa_in", [P, 3, DIM])
    b1_in = sb("b1_in", [EXPERTS * FT, P])
    q_ln = sb("q_ln", [P, 2])
    kv_ln = sb("kv_ln", [P, KV_LORA])
    wqn = sb("wqn", [P, 2, 2, Q_LORA])
    wqr = sb("wqr", [ROPE, 2, 2, Q_LORA])
    wkv = sb("wkv", [P, 2, 2, 2, KV_LORA])
    wo_in = sb("wo_in", [P, 2, KD, 2 * VDIM])
    wot = sb("wot", [P, 2, 2, DIM])
    norm_bank = [bank[0:2], bank[2:4]]
    query_bank, turn_bank, output_bank = bank[4:6], bank[6], bank[7]
    SMALL = 9
    PW = 2 * HW

    s_x = [sem("x_loaded_even"), sem("x_loaded_odd")]
    s_w = [sem("pair_weights_loaded_even"), sem("pair_weights_loaded_odd")]
    s_small = sem("small_weights_loaded")
    s_const = sem("constants_made")
    s_dve = sem("statistics_ready")
    s_var = sem("variance_ready")
    s_eps = sem("eps_added")
    s_rstd = sem("rstd_ready")
    s_xn = sem("xn_ready")
    s_tr = sem("transposes_done")
    s_hi = sem("transpose_hi_copied")
    s_lo = sem("transpose_lo_copied")
    s_passed = sem("waits_passed")
    s_gain = sem("gain_applied")
    s_query = sem("query_weights_made")
    s_query_hi = sem("query_weights_hi_copied")
    s_query_free = sem("query_bank_free")
    s_turned = sem("output_weights_turned")
    s_wot = sem("turned_output_weights_copied")
    s_output = sem("output_weights_made")
    s_output_hi = sem("output_weights_hi_copied")
    s_output_free = sem("output_bank_free")
    s_job = sem("down_projection_or_bias_turned")
    s_job_hi = sem("down_projection_hi_copied")
    s_job_free = sem("down_projection_split")

    q_b_rows = q_b_w.rearrange("(h f) r -> f h r", f=QK)
    kv_b_rows = kv_b_w.rearrange("(h v p) r -> p h v r", v=2, p=P)
    o_rows = o_w.rearrange("(t p) n -> p t n", p=P)

    def steps(engine, step, between=None):
        with engine.Fori(0, BATCH // 2 - 1) as i:
            for odd in range(2):
                step(2 * i + odd, odd, False)
        step(BATCH - 2, 0, False)
        if between is not None:
            between()
        step(BATCH - 1, 1, True)

    def down_bank(n):
        return (query_bank[1], turn_bank, output_bank)[n]

    with nc.Block() as block:

        @block.sync
        def _(sp):
            def step(b, odd, last):
                sp.wait_ge(s_xn, b + 1)
                sp.dma_start(x_in[:, odd], x[bass.ds(b * SEQ, SEQ), :].rearrange("(t p) d -> p t d", p=P)) \
                    .then_inc(s_x[odd], 16)
                sp.wait_ge(s_output, b + 1)
                pair = bass.ds(2 * b, 2)
                sp.dma_start(wqn[:, odd], q_b_rows[0:NOPE, pair]).then_inc(s_w[odd], 16)
                sp.dma_start(wqr[:, odd], q_b_rows[NOPE:QK, pair]).then_inc(s_w[odd], 16)
                sp.dma_start(wkv[:, odd], kv_b_rows[:, pair]).then_inc(s_w[odd], 16)
                sp.dma_start(wo_in[:, odd], o_rows[:, :, bass.ds(b * 2 * VDIM, 2 * VDIM)]).then_inc(s_w[odd], 16)

            steps(sp, step)
            sp.dma_start(pre["w1_in"][:, 0], w1.rearrange("e (k p) f -> p e k f", p=P)[:, 0]).then_inc(pre["s_w1"], 16)
            sp.dma_start(pre["w2_in"][:, :, :], w2.rearrange("e (k p) n -> p e k n", p=P)[:, 0]) \
                .then_inc(pre["s_w2"], 16)
            sp.dma_start(pre["b2_all"][:, :, :], b2.unsqueeze(0).to_broadcast([P, EXPERTS, DIM])) \
                .then_inc(pre["s_b2"], 16)

        @block.gpsimd
        def _(pool):
            pool.memset(ident[:], 0.0).then_inc(s_const, 1)
            pool.memset(mask[:], 0.0).then_inc(s_const, 1)
            pool.memset(minus_half[:], -0.5).then_inc(s_const, 1)
            pool.wait_ge(s_const, 3)
            pool.affine_select(out=ident[:], in_=ident[:], compare_op=ALU.not_equal, fill=1.0, base=0,
                               pattern=[[-1, P]], channel_multiplier=1).then_inc(s_const, 1)
            pool.affine_select(out=mask[:, SEQ - P:], in_=mask[:, SEQ - P:], compare_op=ALU.is_ge, fill=NEG,
                               base=0, pattern=[[-1, P]], channel_multiplier=1).then_inc(s_const, 1)

            def step(b, odd, last):
                pool.wait_ge(s_var, b + 1)
                pool.sem_inc(s_passed, 1)
                pool.tensor_scalar(rstd[:], mean_var[:, :, 1], LN_EPS, None, ALU.add).then_inc(s_eps, 1)
                pool.wait_ge(s_eps, b + 1)
                pool.tensor_tensor(rstd[:], rstd[:], minus_half[:, 0:TILES], ALU.pow).then_inc(s_rstd, 1)
                pool.wait_ge(s_small, 16 * SMALL)
                pool.wait_ge(s_w[odd], 64 * (b // 2 + 1))
                w = wkv[:, odd].rearrange("p h v r -> p (h v) r")
                pool.tensor_tensor(w, w, kv_ln[:, :].unsqueeze(1).to_broadcast([P, 4, KV_LORA]),
                                   ALU.mult).then_inc(s_gain, 1)

            steps(pool, step)

        @block.scalar
        def _(act):
            small = (
                (q_ln[:, 0:1], q_a_ln[0:P].unsqueeze(1)),
                (q_ln[0:64, 1:2], q_a_ln[P:Q_LORA].unsqueeze(1)),
                (q_ln[64:P, 1:2], q_a_ln[P:Q_LORA].unsqueeze(1)),
                (kv_ln[:, :], kv_a_ln.unsqueeze(0).to_broadcast([P, KV_LORA])),
                (wa_in[:, 0, :], q_a_w[0:P, :]),
                (wa_in[0:Q_LORA - P, 1, :], q_a_w[P:Q_LORA, :]),
                (wa_in[Q_LORA - P:P, 1, :], kv_a_w[0:KV_LORA, :]),
                (wa_in[0:ROPE, 2, :], kv_a_w[KV_LORA:KV_LORA + ROPE, :]),
                (b1_in[:, :], b1.rearrange("e (k p) -> (e k) p", p=P)),
            )
            assert len(small) == SMALL
            for dst, src in small:
                act.dma_start(dst, src).then_inc(s_small, 16)
            act.wait_ge(s_small, 16 * SMALL)

            def step(b, odd, last):
                act.wait_ge(s_query, b + 1)
                for i in range(2):
                    ins = act.activation(keep["wq_h"][:, i, bass.ds(b * PW, PW)],
                                         query_bank[odd][:, i * PW:(i + 1) * PW], ACT.Copy, scale=q_ln[:, i:i + 1])
                ins.then_inc(s_query_hi, 1)
                for k in range(KD):
                    act.wait_ge(s_tr, KD * b + k + 1)
                    act.copy(xt_h[:, k, bass.ds(b * SEQ, SEQ)], norm_bank[odd][k][:, :]).then_inc(s_hi, 1)
                act.wait_ge(s_output, 2 + b + 1)
                act.activation(keep["wo_h"][:, bass.ds(b, 1), :], output_bank[:, 0:DIM].unsqueeze(1), ACT.Copy,
                               scale=1.0 / (P_SCALE * C_SCALE)).then_inc(s_output_hi, 1)

            def down():
                for k in range(KD):
                    act.wait_ge(s_job, k + 1)
                    act.copy(keep["wa_h"][:, k, :], down_bank(k)[:, 0:LATENT]).then_inc(s_job_hi, 1)

            steps(act, step, down)

        @block.vector
        def _(dve):
            for free, count in ((s_xn, 2), (s_lo, 2 * KD), (s_query_free, 2), (s_output, 2), (s_wot, 1),
                                (s_output_free, 1)):
                dve.sem_inc(free, count)

            def statistics(b, odd):
                dve.wait_ge(s_x[odd], 16 * (b // 2 + 1))
                for t in range(TILES):
                    ins = dve.bn_stats(stats[:, t, :], x_in[:, odd, t, :])
                ins.then_inc(s_dve, 1)
                dve.wait_ge(s_dve, b + 1)
                dve.sem_inc(s_passed, 1)
                for t in range(TILES):
                    ins = dve.bn_aggr(mean_var[:, t, :], stats[:, t, :])
                ins.then_inc(s_var, 1)

            def step(b, odd, last):
                dve.wait_ge(s_var, b + 1)
                dve.wait_ge(s_rstd, b + 1)
                for t in range(TILES):
                    ins = dve.tensor_scalar(xn[:, t, :], x_in[:, odd, t, :], mean_var[:, t, 0:1], rstd[:, t:t + 1],
                                            ALU.subtract, ALU.mult)
                ins.then_inc(s_xn, 1)
                if not last:
                    statistics(b + 1, 1 - odd)
                dve.wait_ge(s_query_hi, b + 1)
                for i in range(2):
                    cols = bass.ds(b * PW, PW)
                    ins = dve.scalar_tensor_tensor(keep["wq_l"][:, i, cols], query_bank[odd][:, i * PW:(i + 1) * PW],
                                                   q_ln[:, i:i + 1], fp(keep["wq_h"][:, i, cols]), ALU.mult,
                                                   ALU.subtract)
                ins.then_inc(s_query_free, 1)
                dve.wait_ge(s_turned, b + 1)
                dve.tensor_copy(wot[:, odd, :, :], turn_bank[:, :].rearrange("p (h n) -> p h n", h=2)) \
                    .then_inc(s_wot, 1)
                for k in range(KD):
                    dve.wait_ge(s_hi, KD * b + k + 1)
                    dve.tensor_tensor(xt_l[:, k, bass.ds(b * SEQ, SEQ)], norm_bank[odd][k][:, :],
                                      fp(xt_h[:, k, bass.ds(b * SEQ, SEQ)]), ALU.subtract).then_inc(s_lo, 1)
                dve.wait_ge(s_output_hi, b + 1)
                dve.scalar_tensor_tensor(keep["wo_l"][:, bass.ds(b, 1), :], output_bank[:, 0:DIM].unsqueeze(1),
                                         1.0 / (P_SCALE * C_SCALE), fp(keep["wo_h"][:, bass.ds(b, 1), :]), ALU.mult,
                                         ALU.subtract).then_inc(s_output_free, 1)

            def down():
                for k in range(KD):
                    dve.wait_ge(s_job_hi, k + 1)
                    dve.tensor_tensor(keep["wa_l"][:, k, :], down_bank(k)[:, 0:LATENT], fp(keep["wa_h"][:, k, :]),
                                      ALU.subtract).then_inc(s_job_free, 1)
                dve.wait_ge(s_job, KD + 1)
                dve.tensor_copy(keep["b1t"][:, :], down_bank(KD)[:, 0:EXPERTS * FT]).then_inc(s_job_free, 1)

            statistics(0, 0)
            dve.wait_ge(s_small, 16 * SMALL)
            steps(dve, step, down)

        @block.tensor
        def _(pe):
            def step(b, odd, last):
                pe.wait_ge(s_w[odd], 64 * (b // 2 + 1))
                pe.wait_ge(s_gain, b + 1)
                pe.wait_ge(s_query_free, b + 1)
                if last:
                    pe.wait_ge(s_job_free, KD + 1)
                for i, rows, out_rows in ((0, slice(0, P), slice(0, P)), (1, slice(P, Q_LORA), slice(0, 64)),
                                          (1, slice(P, Q_LORA), slice(64, P))):
                    for hh in range(2):
                        c = i * PW + hh * HW
                        pe.matmul(query_bank[odd][out_rows, c:c + KV_LORA], wqn[:, odd, hh, rows],
                                  wkv[:, odd, hh, 0, :], start=True, stop=True)
                        ins = pe.matmul(query_bank[odd][out_rows, c + KV_LORA:c + HW], wqr[:, odd, hh, rows],
                                        ident[0:ROPE, 0:ROPE], start=True, stop=True)
                ins.then_inc(s_query, 1)
                pe.wait_ge(s_wot, b + 1)
                for hh in range(2):
                    for k in range(KD):
                        ins = pe.transpose(turn_bank[:, hh * DIM + k * P:hh * DIM + (k + 1) * P],
                                           wo_in[:, odd, k, hh * VDIM:(hh + 1) * VDIM], ident[:, :])
                ins.then_inc(s_turned, 1)
                pe.wait_ge(s_xn, 2 + b + 1)
                for k in range(KD):
                    pe.wait_ge(s_lo, KD * b + k + 1)
                    for t in range(TILES):
                        ins = pe.transpose(norm_bank[odd][k][:, t * P:(t + 1) * P], xn[:, t, k * P:(k + 1) * P],
                                           ident[:, :])
                    ins.then_inc(s_tr, 1)
                pe.wait_ge(s_wot, 1 + b + 1)
                pe.wait_ge(s_output_free, b + 1)
                for hh in range(2):
                    ins = pe.matmul(output_bank[hh * 64:hh * 64 + 64, 0:DIM], wkv[:, odd, hh, 1, :],
                                    wot[:, odd, hh, :], start=True, stop=True)
                ins.then_inc(s_output, 1)

            def down():
                pe.wait_ge(s_small, 16 * SMALL)
                pe.wait_ge(s_query_free, 2 + BATCH - 2)
                for k in range(KD):
                    if k == 1:
                        pe.wait_ge(s_wot, 1 + BATCH - 1)
                    for i, rows in enumerate((P, P, ROPE)):
                        ins = pe.transpose(down_bank(k)[:, i * P:i * P + rows], wa_in[0:rows, i, k * P:(k + 1) * P],
                                           ident[0:rows, 0:rows])
                    ins.then_inc(s_job, 1)
                pe.wait_ge(s_output_free, 1 + BATCH - 1)
                pe.transpose(down_bank(KD)[:, 0:EXPERTS * FT], b1_in[:, :], ident[0:EXPERTS * FT, 0:EXPERTS * FT]) \
                    .then_inc(s_job, 1)

            pe.wait_ge(s_const, 5)
            steps(pe, step, down)


def experts(nc, own, bank, keep, pre, xt_h, xt_l, xt_dram, z_dram, w1, w2):
    def sb(name, shape, dt=FP32):
        return own.enter_context(nc.sbuf_tensor(name, shape, dt))

    def sem(name):
        return own.enter_context(nc.semaphore(name))

    w1_in, w2_in, b2_all = pre["w1_in"], pre["w2_in"], pre["b2_all"]
    w1_h, w1_l = sb("w1_h", [P, KD, FF], FP32R), sb("w1_l", [P, KD, FF], FP32R)
    w2_h, w2_l = sb("w2_h", [P, FT, DIM], FP32R), sb("w2_l", [P, FT, DIM], FP32R)
    gelu = sb("gelu", [P, 2, CAP * BATCH])
    act_h = sb("act_h", [P, 4, CAP * BATCH], FP32R)
    act_l = sb("act_l", [P, 4, CAP * BATCH], FP32R)
    z = sb("z", [P, TILES, DIM])
    up = bank[0:4]
    down = bank[4:8]
    LAG = 2

    s_w1, s_w2, s_b2 = pre["s_w1"], pre["s_w2"], pre["s_b2"]
    s_xt = sem("tokens_stored")
    s_w1h = sem("w1_hi_made")
    s_w2h = sem("w2_hi_made")
    s_w1s = sem("w1_split")
    s_w2s = sem("w2_split")
    s_up = sem("up_product_done")
    s_gelu = sem("gelu_done")
    s_act = sem("activation_split")
    s_act_h = sem("activation_hi_made")
    s_down = sem("down_product_step_done")
    s_z = sem("z_ready")
    s_zst = sem("z_stored")

    w1_rows = w1.rearrange("e (k p) f -> p e k f", p=P)
    w2_rows = w2.rearrange("e (k p) n -> p e k n", p=P)
    z_rows = z_dram.rearrange("(q o e c) d -> o c e q d", o=2, e=EXPERTS, c=CAP)

    with nc.Block() as block:

        @block.sync
        def _(sp):
            sp.wait_ge(s_w1, 16)
            sp.dma_start(w1_in[:, 1], w1_rows[:, 1]).then_inc(s_w1, 16)
            sp.wait_ge(s_w2s, FT)
            sp.dma_start(w2_in[:, :, :], w2_rows[:, 1]).then_inc(s_w2, 16)
            sp.sem_inc(s_zst, 32)

            def load(e):
                sp.wait_ge(s_w1, 16 * (e + 2))
                sp.wait_ge(s_w1s, FT * (e + 1))
                sp.dma_start(w1_in[:, bass.ds(e % 2, 1)].rearrange("p o k f -> p (o k) f"),
                             w1_rows[:, bass.ds((e + 2) % EXPERTS, 1)].rearrange("p e k f -> p (e k) f")) \
                    .then_inc(s_w1, 16)
                sp.wait_ge(s_w2s, FT * (e + 2))
                sp.dma_start(w2_in[:, :, :], w2_rows[:, bass.ds((e + 2) % EXPERTS, 1)]
                             .rearrange("p e k n -> p (e k) n")).then_inc(s_w2, 16)

            def store(e):
                for part, xt in enumerate((xt_h, xt_l)):
                    sp.dma_start(xt_dram[:, part, :, bass.ds(e * SEQ, SEQ)], fp(xt[:, :, bass.ds(e * SEQ, SEQ)])) \
                        .then_inc(s_xt, 16)
                sp.wait_ge(s_z, TILES * (e + 2))
                for o in range(2):
                    sp.dma_start(z_rows[o][:, bass.ds(e, 1)].rearrange("c e q d -> c (e q) d"),
                                 z[o * CAP:(o + 1) * CAP, :, :]).then_inc(s_zst, 16)

            with sp.Fori(0, EXPERTS - 1) as e:
                load(e)
                store(e)
            store(EXPERTS - 1)
            sp.wait_ge(s_w1, 16 * (EXPERTS + 1))
            sp.wait_ge(s_w2, 16 * (EXPERTS + 1))
            sp.wait_ge(s_zst, 32 * (EXPERTS + 1))
            sp.wait_ge(s_xt, 32 * EXPERTS)

        def w1_tile(w, k):
            return w[:, :, k * P:(k + 1) * P]

        def w1_loaded(e, k):
            return w1_in[:, bass.ds(e % 2, 1), :, k * P:(k + 1) * P]

        @block.scalar
        def _(act):
            def split_w1(e, k):
                act.wait_ge(s_w1, 16 * (e + 1))
                act.copy(w1_tile(w1_h, k).unsqueeze(1), w1_loaded(e, k)).then_inc(s_w1h, 1)

            def split_w2(loads, k):
                act.wait_ge(s_w2, 16 * loads)
                act.copy(w2_h[:, k, :], w2_in[:, k, :]).then_inc(s_w2h, 1)

            act.sem_inc(s_gelu, 4)
            for k in range(FT):
                split_w1(0, k)
            for k in range(FT):
                split_w2(1, k)
            with act.Fori(0, EXPERTS) as e:
                for k in range(FT + LAG + 1):
                    if k < FT:
                        act.wait_ge(s_up, FT * e + k + 1)
                        act.wait_ge(s_act, FT * e + k + 1)
                        act.activation(gelu[:, k % 2, :], up[k % 4][:, :], ACT.Gelu,
                                       bias=keep["b1t"][:, bass.ds(e * FT + k, 1)]).then_inc(s_gelu, 1)
                        split_w1(e + 1, k)
                    if k > LAG:
                        act.wait_ge(s_down, 4 + FT * e + k - LAG)
                        split_w2(e + 2, k - LAG - 1)

        @block.vector
        def _(dve):
            def split_w1(e, k):
                dve.wait_ge(s_w1h, FT * e + k + 1)
                dve.tensor_tensor(w1_tile(w1_l, k).unsqueeze(1), w1_loaded(e, k), fp(w1_tile(w1_h, k)).unsqueeze(1),
                                  ALU.subtract).then_inc(s_w1s, 1)

            def split_w2(done, k):
                dve.wait_ge(s_w2h, done + k + 1)
                dve.tensor_tensor(w2_l[:, k, :], w2_in[:, k, :], fp(w2_h[:, k, :]),
                                  ALU.subtract).then_inc(s_w2s, 1)

            dve.sem_inc(s_act, 2)
            dve.sem_inc(s_z, TILES)
            for k in range(FT):
                split_w1(0, k)
            for k in range(FT):
                split_w2(0, k)
            dve.wait_ge(s_b2, 16)
            with dve.Fori(0, EXPERTS) as e:
                for k in range(FT + LAG + 1):
                    if k < FT:
                        dve.wait_ge(s_gelu, 4 + FT * e + k + 1)
                        dve.wait_ge(s_down, FT * e + k + 1)
                        dve.tensor_copy(act_h[:, k % 4, :], gelu[:, k % 2, :]).then_inc(s_act_h, 1)
                        dve.wait_ge(s_act_h, FT * e + k + 1)
                        dve.tensor_tensor(act_l[:, k % 4, :], gelu[:, k % 2, :], fp(act_h[:, k % 4, :]),
                                          ALU.subtract).then_inc(s_act, 1)
                        split_w1(e + 1, k)
                    if k > LAG:
                        split_w2(FT * (e + 1), k - LAG - 1)
                dve.wait_ge(s_down, 4 + FT * (e + 1))
                dve.wait_ge(s_zst, 32 * (e + 1))
                for t in range(TILES):
                    dve.tensor_tensor(z[:, t:t + 1, :], down[t][:, 0:DIM].unsqueeze(1),
                                      b2_all[:, bass.ds(e, 1), :], ALU.add).then_inc(s_z, 1)

        @block.tensor
        def _(pe):
            pe.sem_inc(s_down, 4)
            x_h = xt_h[:, :, :].rearrange("p k (b s) -> p k b s", s=SEQ)
            x_l = xt_l[:, :, :].rearrange("p k (b s) -> p k b s", s=SEQ)
            with pe.Fori(0, EXPERTS) as e:
                for k in range(FT + LAG):
                    if k < FT:
                        pe.wait_ge(s_w1s, FT * e + k + 1)
                        pe.wait_ge(s_gelu, FT * e + k + 1)
                        ps = up[k % 4][:, :].rearrange("p (b c) -> p b c", c=CAP)
                        n = 0
                        for d in range(KD):
                            for w, xx in ((w1_h, x_h), (w1_l, x_h), (w1_h, x_l)):
                                ins = pe.matmul(ps, w[:, d, k * P:(k + 1) * P], xx[:, d, :, bass.ds(e * CAP, CAP)],
                                                start=(n == 0), stop=(n == 3 * KD - 1))
                                n += 1
                        ins.then_inc(s_up, 1)
                    if k >= LAG:
                        j = k - LAG
                        pe.wait_ge(s_act, 2 + FT * e + j + 1)
                        pe.wait_ge(s_w2s, FT * e + j + 1)
                        if j == 0:
                            pe.wait_ge(s_z, TILES * (e + 1))
                        for t in range(TILES):
                            cols = slice(t * P, (t + 1) * P)
                            n = 0
                            for a, w in ((act_h, w2_h), (act_h, w2_l), (act_l, w2_h)):
                                ins = pe.matmul(down[t][:, 0:DIM], a[:, j % 4, cols], w[:, j, :],
                                                start=(j == 0 and n == 0), stop=(j == FT - 1 and n == 2))
                                n += 1
                        ins.then_inc(s_down, 1)


def attend(nc, own, bank, keep, xt_dram, z_dram, x, cos_t, sin_t, out):
    def sb(name, shape, dt=FP32):
        return own.enter_context(nc.sbuf_tensor(name, shape, dt))

    def sem(name):
        return own.enter_context(nc.semaphore(name))

    ident, mask = keep["ident"], keep["mask"]

    cos, sin = sb("cos", [P, TILES, ROPE]), sb("sin", [P, TILES, ROPE])
    xs = sb("xs", [P, 2, KD, SEQ], FP32R)
    raw = sb("raw", [P, 2, LATENT])
    mean_sq = sb("mean_sq", [P, 2, 2])
    rms = sb("rms", [P, 2, 2])
    q_lat = sb("q_lat", [P, 2, 2 * P])
    keys = sb("keys", [P, 2, HW])
    turn = sb("turn", [P, 2, 2, ROPE])
    qlt_h = sb("qlt_h", [P, 2, SEQ], FP32R)
    qlt_l = sb("qlt_l", [P, SEQ], FP32R)
    keyt_h = sb("keyt_h", [P, 2, SEQ], FP32R)
    keyt_l = sb("keyt_l", [P, 2, SEQ], FP32R)
    lat = sb("lat", [P, 2 * TILES, 2, KV_LORA], FP16)
    q_tok = sb("q_tok", [P, TILES, GH, HW])
    q_turn = sb("q_turn", [P, 2, GH, ROPE])
    qt_h = sb("qt_h", [P, 2, GH, SEQ], FP32R)
    qt_l = sb("qt_l", [P, 2, GH, SEQ], FP32R)
    scores = sb("scores", [P, 2, SEQ])
    neg_max = sb("neg_max", [P, 2])
    probs = sb("probs", [P, 4, SEQ])
    sums = sb("sums", [P, 2, TILES])
    inv_sums = sb("inv_sums", [P, 2, TILES])
    pt_h = sb("pt_h", [P, 4, TILES, P], FP16)
    pt_l = sb("pt_l", [P, 4, TILES, P], FP16)
    mixed2 = sb("mixed2", [P, 2, TILES, 2, KV_LORA])
    mixed = sb("mixed", [P, 2, TILES, 2 * KV_LORA])
    mt_h = sb("mt_h", [P, PAIRS, SEQ], FP32R)
    mt_l = sb("mt_l", [P, PAIRS, SEQ], FP32R)
    x_res = sb("x_res", [P, TILES, DIM])
    gate = sb("gate", [P, TILES, DIM])
    tanh = sb("tanh", [P, TILES, DIM])
    result = sb("result", [P, TILES, DIM])

    score_bank, turned_bank, mix_bank, work_bank = bank[0:2], bank[2:4], bank[4:6], bank[6:8]
    out_bank = bank[0:4]

    s_rope = sem("rotation_tables_loaded")
    s_xs = sem("tokens_loaded")
    s_res = sem("residual_and_gate_loaded")
    s_tanh = sem("tanh_ready")
    s_result = sem("result_ready")
    s_stored = sem("result_stored")
    s_projected = sem("output_projected")
    s_projected_free = sem("output_bank_free")
    s_scores = sem("score_bank_ready")
    s_scores_free = sem("score_bank_free")
    s_probs = sem("probs_ready")
    s_turned = sem("probs_transposed")
    s_pt_h = sem("probs_hi_copied")
    s_pt = sem("probs_split")
    s_mix = sem("mix_step_done")
    s_inv = sem("inverse_sums_ready")
    s_mix_free = sem("mix_bank_free")
    s_mixed = sem("head_mixed")
    s_work = sem("work_bank_ready")
    s_work_hi = sem("work_bank_copied_by_scalar")
    s_work_free = sem("work_bank_free")
    s_eps = sem("rms_eps_added")
    s_rms = sem("rms_ready")
    s_keys = sem("latents_normed")
    s_turn = sem("key_rotation_products_ready")
    s_split = sem("latents_hi_made")
    s_qturn = sem("query_rotation_products_ready")
    s_qtok = sem("queries_turned")
    s_passed = sem("waits_passed")

    NEXT = [("latent", 0), ("latent", 1), ("flip", 0), ("latent", 2), ("flip", 1), ("latent", 3), ("flip", 2),
            ("flip", 3)] + [("query", (0, t)) for t in range(TILES)] + [("queryT", (0, j)) for j in range(GH)]
    plan = {step: ("mixedT", j) for j, step in enumerate(MIXED_TURN_STEPS)}
    for g in range(1, GROUPS):
        for steps, kind in ((QUERY_STEPS[g - 1], "query"), (QUERY_TURN_STEPS[g - 1], "queryT")):
            for i, step in enumerate(steps):
                assert step not in plan
                plan[step] = (kind, (g, i))
    for step, job in NEXT_STEPS:
        assert step not in plan
        plan[step] = job
    TAIL = [("mixedT", PAIRS - 1)] + [job for job in NEXT if job not in plan.values()]
    beside = {step: (n, *plan[step]) for n, step in enumerate(sorted(plan))}
    order = [plan[step] for step in sorted(plan)] + TAIL
    JOBS, FIRST, TAIL_AT = len(order), len(NEXT), len(plan)
    LAG_T, LAG_M = 3, 5
    STEPS = UNITS + LAG_M + 1
    MIXED_STEPS = [TILES * h + LAG_M + 7 for h in range(HEADS - 1)] + [STEPS - 1]
    assert JOBS % 2 == 0 and FIRST % 2 == 0

    def vector_step(step):
        return step + (LATENT_DELAY if beside[step][1] == "latent" else 1)

    BY_SCALAR = ("latent", "query")
    by_vector = [kind not in BY_SCALAR for kind, _ in order]
    FIRST_FREED, FREED = sum(kind not in BY_SCALAR for kind, _ in NEXT), sum(by_vector)

    def freed_first(n):
        return sum(kind not in BY_SCALAR for kind, _ in NEXT[:n])

    def freed(b, n):
        return FIRST_FREED + FREED * b + sum(by_vector[:n])

    def queries_freed(b, g, j):
        return freed(b, 0) if g == 0 else freed(b, 1 + order.index(("queryT", (g, j))))

    def queries_done(b, g):
        return TILES * (GROUPS * b + (g - 1) % GROUPS + 1)

    def keys_of(u):
        return (u % TILES + 1) * P

    with nc.Block() as block:

        @block.sync
        def _(sp):
            sp.sem_inc(s_stored, 16)
            for part in range(2):
                sp.dma_start(fp(xs[:, part, :, :]), xt_dram[:, part, :, 0:SEQ]).then_inc(s_xs, 16)
            for table, values in ((cos, cos_t), (sin, sin_t)):
                sp.dma_start(table[:, :, :], values.rearrange("(t p) f -> p t f", p=P)).then_inc(s_rope, 16)
            with sp.Fori(0, BATCH) as b:
                rows = bass.ds(b * SEQ, SEQ)
                sp.wait_ge(s_result, TILES * (b + 1))
                sp.dma_start(x_res[:, :, :], x[rows, :].rearrange("(t p) d -> p t d", p=P)).then_inc(s_res, 16)
                sp.dma_start(gate[:, :, :], z_dram[rows, :].rearrange("(t p) d -> p t d", p=P)).then_inc(s_res, 16)
                sp.wait_ge(s_work, FIRST + JOBS * b)
                for part in range(2):
                    sp.dma_start(fp(xs[:, part, :, :]), xt_dram[:, part, :, bass.ds((b + 1) % BATCH * SEQ, SEQ)]) \
                        .then_inc(s_xs, 16)
                sp.wait_ge(s_result, TILES * (b + 2))
                sp.dma_start(out[rows, :].rearrange("(t p) d -> p t d", p=P), result[:, :, :]).then_inc(s_stored, 16)
            sp.wait_ge(s_xs, 32 * (BATCH + 1))
            sp.wait_ge(s_stored, 16 * (BATCH + 1))

        @block.gpsimd
        def _(pool):
            def latent(job, done, t):
                pool.wait_ge(s_work_hi, job + 1)
                pool.sem_inc(s_passed, 1)
                pool.tensor_scalar(rms[:, t % 2, :], mean_sq[:, t % 2, :], RMS_EPS, None, ALU.add).then_inc(s_eps, 1)
                pool.wait_ge(s_eps, done + t + 1)
                pool.tensor_tensor(rms[:, t % 2, :], rms[:, t % 2, :], keep["minus_half"][:, 0:2],
                                   ALU.pow).then_inc(s_rms, 1)

            def query(job, done, t):
                pool.wait_ge(s_work_hi, job + 1)
                pool.wait_ge(s_qtok, done + t + 1)
                src = q_tok[:, t, :, KV_LORA:]
                pool.tensor_tensor(q_turn[:, 0], src, cos[:, t, :].unsqueeze(1).to_broadcast([P, GH, ROPE]),
                                   ALU.mult)
                pool.tensor_tensor(q_turn[:, 1].rearrange("p h (a f) -> p h a f", a=2),
                                   src.rearrange("p h (a f) -> p h a f", a=2)[:, :, ::-1, :],
                                   sin[:, t, :].rearrange("p (a f) -> p a f", a=2).unsqueeze(1)
                                   .to_broadcast([P, GH, 2, ROPE // 2]), ALU.mult).then_inc(s_qturn, 1)
                pool.wait_ge(s_qturn, done + t + 1)
                pool.tensor_tensor(src, q_turn[:, 0], q_turn[:, 1], ALU.add).then_inc(s_qtok, 1)

            pool.sem_inc(s_qtok, 1)
            pool.wait_ge(s_rope, 32)
            pool.sem_inc(s_mixed, 2)
            for n, (kind, at) in enumerate(NEXT):
                if kind == "latent":
                    latent(n, 0, at)
                elif kind == "query":
                    query(n, 0, at[1])
            with pool.Fori(0, BATCH) as b:
                for s in range(STEPS):
                    if s in beside:
                        n, kind, at = beside[s]
                        if kind == "latent":
                            latent(FIRST + JOBS * b + n, TILES * (b + 1), at)
                        elif kind == "query":
                            query(FIRST + JOBS * b + n, queries_done(b, at[0]), at[1])
                    if s in MIXED_STEPS:
                        h = MIXED_STEPS.index(s)
                        pool.wait_ge(s_mix_free, 2 + HEADS * b + h + 1)
                        pool.tensor_tensor(mixed[:, h // 2 % 2, :, h % 2 * KV_LORA:(h % 2 + 1) * KV_LORA], mixed2[:, h % 2, :, 0, :],
                                           mixed2[:, h % 2, :, 1, :], ALU.add).then_inc(s_mixed, 1)

        @block.scalar
        def _(act):
            def take(index, n, kind, at, par):
                act.wait_ge(s_work, index + 1)
                ps = work_bank[n % 2]
                if kind == "latent":
                    act.copy(raw[:, at % 2, :], ps[:, 0:LATENT])
                    act.activation(q_lat[:, at % 2, 0:Q_LORA], ps[:, 0:Q_LORA], ACT.Square,
                                   scale=float(Q_LORA) ** -0.5, accum_out=mean_sq[:, at % 2, 0:1])
                    ins = act.activation(q_lat[:, at % 2, Q_LORA:], ps[:, Q_LORA:Q_LORA + KV_LORA], ACT.Square,
                                         scale=float(KV_LORA) ** -0.5, accum_out=mean_sq[:, at % 2, 1:2])
                elif kind == "flip":
                    cols = slice(at * P, (at + 1) * P)
                    act.copy(qlt_h[:, :, cols], ps[:, 0:2 * P].rearrange("p (a c) -> p a c", a=2))
                    ins = act.copy(keyt_h[:, bass.ds(par, 1), cols], ps[:, 2 * P:3 * P].unsqueeze(1))
                elif kind == "query":
                    g, t = at
                    ins = act.copy(q_tok[:, t, :, :], ps[:, :].rearrange("p (h f) -> p h f", h=GH))
                elif kind == "queryT":
                    g, j = at
                    ins = act.copy(qt_h[:, g % 2, j, :], ps[:, :])
                else:
                    ins = act.copy(mt_h[:, at, :], ps[:, :])
                ins.then_inc(s_work_hi, 1)

            act.sem_inc(s_probs, 2)
            for n, (kind, at) in enumerate(NEXT):
                take(n, n, kind, at, 0)
            with act.Fori(0, BATCH) as b:
                for s in range(STEPS):
                    u = s - LAG_T
                    if 0 <= u < UNITS:
                        act.wait_ge(s_turned, 4 + UNITS * b + u + 1)
                        act.wait_ge(s_mix, UNITS * b + u + 1)
                        m = u % TILES + 1
                        act.activation(pt_h[:, u % 4, 0:m, :],
                                       turned_bank[u % 2][:, 0:m * P].rearrange("p (m c) -> p m c", c=P),
                                       ACT.Copy, scale=P_SCALE).then_inc(s_pt_h, 1)
                    if s < UNITS:
                        act.wait_ge(s_scores_free, 2 + UNITS * b + s + 1)
                        act.wait_ge(s_turned, UNITS * b + s + 1)
                        act.activation(probs[:, s % 4, 0:keys_of(s)], scores[:, s % 2, 0:keys_of(s)], ACT.Exp,
                                       scale=-1.0, bias=neg_max[:, s % 2:s % 2 + 1],
                                       accum_out=sums[:, s // TILES % 2, s % TILES:s % TILES + 1]) \
                            .then_inc(s_probs, 1)
                    if s in beside:
                        n, kind, at = beside[s]
                        take(FIRST + JOBS * b + n, n, kind, at, (b + 1) % 2)
                    if s == UNITS:
                        act.wait_ge(s_res, 32 * (b + 1))
                        act.activation(tanh[:, :, :], gate[:, :, :], ACT.Tanh, scale=0.5).then_inc(s_tanh, 1)
                for n, (kind, at) in enumerate(TAIL, TAIL_AT):
                    take(FIRST + JOBS * b + n, n, kind, at, None)

        @block.vector
        def _(dve):
            def take(index, n, kind, at, par, lat_done):
                ps = work_bank[n % 2]
                if kind == "latent":
                    t = at
                    dve.wait_ge(s_rms, lat_done + t + 1)
                    dve.wait_ge(s_split, lat_done + t + 1)
                    dve.tensor_scalar(q_lat[:, t % 2, 0:Q_LORA], raw[:, t % 2, 0:Q_LORA], rms[:, t % 2, 0:1], None, ALU.mult)
                    dve.tensor_scalar(q_lat[:, t % 2, Q_LORA:], raw[:, t % 2, P:Q_LORA], rms[:, t % 2, 0:1], None, ALU.mult)
                    dve.tensor_scalar(keys[:, t % 2, 0:KV_LORA], raw[:, t % 2, Q_LORA:Q_LORA + KV_LORA],
                                      rms[:, t % 2, 1:2], None, ALU.mult)
                    src = raw[:, t % 2, Q_LORA + KV_LORA:]
                    dve.tensor_tensor(turn[:, t % 2, 0, :], src, cos[:, t, :], ALU.mult)
                    dve.tensor_tensor(turn[:, t % 2, 1, :].rearrange("p (a f) -> p a f", a=2),
                                      src.rearrange("p (a f) -> p a f", a=2)[:, ::-1, :],
                                      sin[:, t, :].rearrange("p (a f) -> p a f", a=2),
                                      ALU.mult).then_inc(s_turn, 1)
                    dve.wait_ge(s_turn, lat_done + t + 1)
                    dve.tensor_tensor(keys[:, t % 2, KV_LORA:], turn[:, t % 2, 0, :], turn[:, t % 2, 1, :],
                                      ALU.add).then_inc(s_keys, 1)
                    row = bass.ds(par * TILES + t, 1)
                    src = keys[:, t % 2, 0:KV_LORA].unsqueeze(1)
                    dve.tensor_scalar(lat[:, row, 0, :], src, C_SCALE, None, ALU.mult).then_inc(s_split, 1)
                    dve.wait_ge(s_split, 1 + lat_done + t + 1)
                    dve.scalar_tensor_tensor(lat[:, row, 1, :], src, C_SCALE, lat[:, row, 0, :], ALU.mult,
                                             ALU.subtract)
                    return
                dve.wait_ge(s_work_hi, index + 1)
                if kind == "flip":
                    cols = slice(at * P, (at + 1) * P)
                    dve.tensor_tensor(qlt_l[:, cols], ps[:, 0:P], fp(qlt_h[:, 0, cols]), ALU.subtract)
                    dve.tensor_tensor(qlt_h[64:P, 1, cols], ps[64:P, P:2 * P], fp(qlt_h[64:P, 1, cols]),
                                      ALU.subtract)
                    ins = dve.tensor_tensor(keyt_l[:, bass.ds(par, 1), cols], ps[:, 2 * P:3 * P].unsqueeze(1),
                                            fp(keyt_h[:, bass.ds(par, 1), cols]), ALU.subtract)
                elif kind == "queryT":
                    g, j = at
                    ins = dve.tensor_tensor(qt_l[:, g % 2, j, :], ps[:, :], fp(qt_h[:, g % 2, j, :]), ALU.subtract)
                else:
                    ins = dve.tensor_tensor(mt_l[:, at, :], ps[:, :], fp(mt_h[:, at, :]), ALU.subtract)
                ins.then_inc(s_work_free, 1)

            dve.wait_ge(s_rope, 32)
            for free, count in ((s_scores_free, 2), (s_pt, 2), (s_mix_free, 2), (s_result, TILES),
                                (s_projected_free, TILES), (s_split, 1)):
                dve.sem_inc(free, count)
            for n, (kind, at) in enumerate(NEXT):
                if kind != "query":
                    take(n, n, kind, at, 0, 0)
            with dve.Fori(0, BATCH) as b:
                def beside_step(s):
                    if s in beside and beside[s][1] != "query":
                        n, kind, at = beside[s]
                        take(FIRST + JOBS * b + n, n, kind, at, (b + 1) % 2, TILES * (b + 1))

                for s in range(STEPS):
                    if s in MIXED_STEPS:
                        h = MIXED_STEPS.index(s)
                        dve.wait_ge(s_mix, 4 + UNITS * b + TILES * (h + 1))
                        dve.wait_ge(s_inv, HEADS * b + h + 1)
                        dve.wait_ge(s_mixed, HEADS * b + h + 1)
                        dve.tensor_tensor(mixed2[:, h % 2], mix_bank[h % 2][:, :]
                                          .rearrange("p (t a c) -> p t a c", a=2, c=KV_LORA),
                                          inv_sums[:, h % 2, :].unsqueeze(2).unsqueeze(3)
                                          .to_broadcast([P, TILES, 2, KV_LORA]), ALU.mult).then_inc(s_mix_free, 1)
                    if s < UNITS:
                        N = keys_of(s)
                        dve.wait_ge(s_scores, UNITS * b + s + 1)
                        dve.wait_ge(s_probs, UNITS * b + s + 1)
                        dve.sem_inc(s_passed, 1)
                        dve.tensor_tensor_reduce(out=scores[:, s % 2, 0:N], in0=score_bank[s % 2][:, 0:N],
                                                 in1=mask[:, SEQ - N:SEQ], scale=-SCALE, scalar=-NEG,
                                                 op0=ALU.add, op1=ALU.min,
                                                 accum_out=neg_max[:, s % 2:s % 2 + 1])\
                            .then_inc(s_scores_free, 1)
                    for step in range(STEPS):
                        if step in beside and vector_step(step) == s:
                            beside_step(step)
                    u = s - LAG_T
                    if 0 <= u < UNITS:
                        m = u % TILES + 1
                        dve.wait_ge(s_pt_h, UNITS * b + u + 1)
                        dve.scalar_tensor_tensor(pt_l[:, u % 4, 0:m, :],
                                                 turned_bank[u % 2][:, 0:m * P].rearrange("p (m c) -> p m c", c=P),
                                                 P_SCALE, pt_h[:, u % 4, 0:m, :], ALU.mult,
                                                 ALU.subtract).then_inc(s_pt, 1)
                    if s % TILES == 2 and 6 <= s < UNITS + 4:
                        h = (s - 6) // TILES
                        dve.wait_ge(s_probs, 2 + UNITS * b + TILES * (h + 1))
                        dve.reciprocal(inv_sums[:, h % 2, :], sums[:, h % 2, :]).then_inc(s_inv, 1)
                    if s == UNITS + 2:
                        dve.wait_ge(s_tanh, b + 1)
                        dve.scalar_tensor_tensor(gate[:, :, :], tanh[:, :, :], 1.0, gate[:, :, :], ALU.add, ALU.mult)

                for n, (kind, at) in enumerate(TAIL, TAIL_AT):
                    take(FIRST + JOBS * b + n, n, kind, at, None, None)
                dve.wait_ge(s_stored, 16 * (b + 1))
                for t in range(TILES):
                    dve.wait_ge(s_projected, TILES * b + t + 1)
                    dve.tensor_tensor(result[:, t, :], out_bank[t][:, 0:DIM], gate[:, t, :],
                                      ALU.mult).then_inc(s_projected_free, 1)
                    dve.wait_ge(s_projected_free, TILES * (b + 1) + t + 1)
                    dve.scalar_tensor_tensor(result[:, t, :], result[:, t, :], 0.5, x_res[:, t, :], ALU.mult,
                                             ALU.add).then_inc(s_result, 1)

        @block.tensor
        def _(pe):
            def three(ps, parts):
                n = 0
                for (a_h, a_l), (w_h, w_l) in parts:
                    for a, w in ((a_h, w_h), (a_h, w_l), (a_l, w_h)):
                        ins = pe.matmul(ps, a, w, start=(n == 0), stop=(n == 3 * len(parts) - 1))
                        n += 1
                return ins

            def make(index, bank_free, n, kind, at, lat_done, q_done, mixed_done=None):
                if bank_free is not None:
                    pe.wait_ge(*bank_free)
                ps = work_bank[n % 2]
                if kind == "latent":
                    if at == 0:
                        pe.wait_ge(s_xs, 32 * (lat_done + 1))
                    cols = slice(at * P, (at + 1) * P)
                    ins = three(ps[:, 0:LATENT],
                                [((xs[:, 0, k, cols], xs[:, 1, k, cols]), (keep["wa_h"][:, k, :], keep["wa_l"][:, k, :]))
                                 for k in range(KD)])
                elif kind == "flip":
                    pe.wait_ge(s_keys, lat_done * TILES + at + 1)
                    pe.transpose(ps[:, 0:P], q_lat[:, at % 2, 0:P], ident[:, :])
                    pe.transpose(ps[:, P:2 * P], q_lat[:, at % 2, P:], ident[:, :])
                    ins = pe.transpose(ps[:, 2 * P:3 * P], keys[:, at % 2, :], ident[:, :])
                elif kind == "query":
                    g, t = at
                    rows, cols = slice(t * P, (t + 1) * P), slice(g * GW, (g + 1) * GW)
                    wq_h, wq_l = keep["wq_h"], keep["wq_l"]
                    pairs = ((qlt_h[:, 0, rows], wq_h[:, 0, cols]), (qlt_h[:, 0, rows], wq_l[:, 0, cols]),
                             (qlt_l[:, rows], wq_h[:, 0, cols]),
                             (qlt_h[:, 1, rows], wq_h[:, 1, cols]), (qlt_h[:, 1, rows], wq_l[:, 1, cols]))
                    for i, (a, w) in enumerate(pairs):
                        ins = pe.matmul(ps[:, :], a, w, start=(i == 0), stop=(i == len(pairs) - 1))
                elif kind == "queryT":
                    g, j = at
                    if j == 0:
                        pe.wait_ge(s_qtok, 1 + q_done + TILES)
                    for t in range(TILES):
                        ins = pe.transpose(ps[:, t * P:(t + 1) * P], q_tok[:, t, j, :], ident[:, :])
                else:
                    pe.wait_ge(s_mixed, mixed_done + 2 * at + 2)
                    for t in range(TILES):
                        ins = pe.transpose(ps[:, t * P:(t + 1) * P], mixed[:, at % 2, t, :], ident[:, :])
                ins.then_inc(s_work, 1)

            pe.sem_inc(s_turned, 4)
            pe.sem_inc(s_mix, 4)
            for n, (kind, at) in enumerate(NEXT):
                bank_free = None
                if n >= 2:
                    bank_free = (s_work_hi, n - 1) if NEXT[n - 2][0] in BY_SCALAR else (s_work_free, freed_first(n - 1))
                make(n, bank_free, n, kind, at, 0, 0)
            with pe.Fori(0, BATCH) as b:
                def bank_free(n):
                    if n >= 2 and not by_vector[n - 2]:
                        return s_work_hi, FIRST + JOBS * b + n - 1
                    return s_work_free, freed(b, n - 1) if n >= 1 else freed(b, 0) - 1

                def q_done(kind, at):
                    return queries_done(b, at[0]) if kind == "queryT" else None

                def project(t, pairs):
                    for j in pairs:
                        rows = slice(t * P, (t + 1) * P)
                        for i, (a, w) in enumerate(((mt_h, "wo_h"), (mt_h, "wo_l"), (mt_l, "wo_h"))):
                            ins = pe.matmul(out_bank[t][:, 0:DIM], a[:, j, rows], keep[w][:, j, :],
                                            start=(j == 0 and i == 0), stop=(j == PAIRS - 1 and i == 2))
                    return ins

                for s in range(STEPS):
                    if s < UNITS:
                        h, t = s // TILES, s % TILES
                        g, j = h // GH, h % GH
                        if t == 0:
                            pe.wait_ge(s_work_free, queries_freed(b, g, j))
                        if s < 2:
                            pe.wait_ge(s_projected_free, TILES * b + s + 1)
                        pe.wait_ge(s_scores_free, UNITS * b + s + 1)
                        N = max(keys_of(s), 2 * P)
                        rows = slice(t * P, (t + 1) * P)
                        par = bass.ds(b % 2, 1)
                        ps = score_bank[s % 2][:, 0:N].unsqueeze(1)
                        three(ps, [((qt_h[:, g % 2, j, rows], qt_l[:, g % 2, j, rows]),
                                          (keyt_h[:, par, 0:N], keyt_l[:, par, 0:N]))]).then_inc(s_scores, 1)
                    u = s - LAG_T
                    if 0 <= u < UNITS:
                        if u < 2:
                            pe.wait_ge(s_projected_free, TILES * b + 2 + u + 1)
                        pe.wait_ge(s_probs, 2 + UNITS * b + u + 1)
                        pe.wait_ge(s_pt, UNITS * b + u + 1)
                        for k in range(u % TILES + 1):
                            ins = pe.transpose(turned_bank[u % 2][:, k * P:(k + 1) * P],
                                               probs[:, u % 4, k * P:(k + 1) * P], ident[:, :])
                        ins.then_inc(s_turned, 1)
                    u = s - LAG_M
                    if 0 <= u < UNITS:
                        h, t = u // TILES, u % TILES
                        pe.wait_ge(s_pt, 2 + UNITS * b + u + 1)
                        if t == 0:
                            pe.wait_ge(s_mix_free, HEADS * b + h + 1)
                        for k in range(t + 1):
                            for i, pt in enumerate((pt_h, pt_l)):
                                ins = pe.matmul(mix_bank[h % 2][:, t * P:(t + 1) * P].unsqueeze(1), pt[:, u % 4, k, :],
                                                lat[:, bass.ds(b % 2 * TILES + k, 1), :, :]
                                                .rearrange("p o a c -> p o (a c)"),
                                                start=(k == 0 and i == 0), stop=(k == t and i == 1))
                        ins.then_inc(s_mix, 1)
                    if s in beside:
                        n, kind, at = beside[s]
                        make(FIRST + JOBS * b + n, bank_free(n), n, kind, at, b + 1, q_done(kind, at), 2 + HEADS * b)
                    t = s - (STEPS - TILES)
                    if t >= 0:
                        if t == 0:
                            pe.wait_ge(s_work_free, freed(b, 1 + order.index(("mixedT", PAIRS - 3))))
                        pe.wait_ge((s_scores_free, s_pt)[t // 2], 2 + UNITS * (b + 1) - 1 + t % 2)
                        project(t, range(PAIRS - 2))
                for n, (kind, at) in enumerate(TAIL, TAIL_AT):
                    make(FIRST + JOBS * b + n, bank_free(n), n, kind, at, None, q_done(kind, at), 2 + HEADS * b)
                pe.wait_ge(s_work_free, freed(b, TAIL_AT))
                for t in range(TILES):
                    project(t, [PAIRS - 2])
                pe.wait_ge(s_work_free, freed(b, TAIL_AT + 1))
                for t in range(TILES):
                    project(t, [PAIRS - 1]).then_inc(s_projected, 1)


_INS = ["L0_attn_hidden_states", "L0_attn_q_a_w", "L0_attn_q_a_ln_w", "L0_attn_q_b_w", "L0_attn_kv_a_w",
        "L0_attn_kv_a_ln_w", "L0_attn_kv_b_w", "L0_attn_o_w", "L0_ffn_w1", "L0_ffn_b1", "L0_ffn_w2", "L0_ffn_b2"]


def rope_tables():
    f32 = np.float32
    inv_freq = f32(1.0) / f32(ROPE_THETA) ** (np.arange(0, ROPE, 2, dtype=f32) / f32(ROPE))
    angle = np.outer(np.arange(SEQ, dtype=f32), inv_freq.astype(f32)).astype(f32)
    cos, sin = np.cos(angle), np.sin(angle)
    return (np.concatenate([cos, cos], axis=-1).astype(f32), np.concatenate([-sin, sin], axis=-1).astype(f32))


def kernel(**inputs):
    import concourse.bacc as bacc
    from concourse.bass_utils import run_bass_kernel_spmd

    nc = bacc.Bacc("TRN2", target_bir_lowering=False, num_devices=1)
    arrays = {name: np.ascontiguousarray(inputs[name]) for name in _INS}
    arrays["L0_attn_hidden_states"] = arrays["L0_attn_hidden_states"].reshape(TOKENS, DIM)
    arrays["cos_table"], arrays["sin_table"] = rope_tables()
    args = [nc.dram_tensor(f"in_{n}", a.shape, mybir.dt.from_np(a.dtype), kind="ExternalInput").ap()
            for n, a in arrays.items()]
    out = nc.dram_tensor("out", (TOKENS, DIM), FP32, kind="ExternalOutput").ap()
    build(nc, *args, out)
    r = run_bass_kernel_spmd(nc, [{f"in_{n}": a for n, a in arrays.items()}], core_ids=[0])
    return r.results[0]["out"].reshape(BATCH, SEQ, DIM)
```

```python
from contextlib import ExitStack

import numpy as np

import concourse.bass as bass
from concourse import mybir

FP32 = mybir.dt.float32
FP32R = mybir.dt.float32r
FP16 = mybir.dt.float16
ALU = mybir.AluOpType
ACT = mybir.ActivationFunctionType

P = 128
BATCH, SEQ, DIM = 8, 512, 256
TOKENS = BATCH * SEQ
HEADS, NOPE, ROPE, VDIM = 16, 128, 64, 128
QK = NOPE + ROPE
Q_LORA, KV_LORA = 192, 64
EXPERTS, FF = 8, 1024
CAP = SEQ // EXPERTS
LN_EPS, RMS_EPS = 1e-5, 1e-6
SCALE = QK ** -0.5
ROPE_THETA = 10000.0

TILES = SEQ // P
KD = DIM // P
GROUPS = 4
GH = HEADS // GROUPS
HW = KV_LORA + ROPE
GW = GH * HW
LATENT = Q_LORA + KV_LORA + ROPE
PAIRS = HEADS // 2
UNITS = HEADS * TILES
FT = FF // P

QUERY_STEPS = ((1, 2, 4, 5), (18, 19, 21, 26), (35, 36, 38, 40))
QUERY_TURN_STEPS = ((11, 13, 15, 16), (29, 32, 33, 34), (45, 49, 50, 51))
LATENT_DELAY = 2
MIXED_TURN_STEPS = (20, 31, 37, 42, 55, 62, 67)
NEXT_STEPS = ((25, ("latent", 0)), (27, ("latent", 1)), (43, ("flip", 0)), (46, ("latent", 2)),
              (48, ("flip", 1)), (52, ("flip", 2)), (53, ("latent", 3)), (54, ("query", (0, 0))),
              (57, ("query", (0, 1))), (58, ("flip", 3)), (59, ("query", (0, 2))), (60, ("query", (0, 3))),
              (63, ("queryT", (0, 0))), (64, ("queryT", (0, 1))), (65, ("queryT", (0, 2))), (68, ("queryT", (0, 3))))

P_SCALE = 2.0 ** 12
C_SCALE = 2.0 ** 8
OUT_SCALE = 0.5 / (P_SCALE * C_SCALE)
NEG = -3.0e38


def fp(ap):
    return ap.bitcast(FP32)


def build(nc, x, q_a_w, q_a_ln, q_b_w, kv_a_w, kv_a_ln, kv_b_w, o_w, w1, b1, w2, b2, cos_t, sin_t, out):
    z_dram = nc.dram_tensor("z_scratch", [TOKENS, DIM], FP32, kind="Internal").ap()
    xt_dram = nc.dram_tensor("xt_scratch", [P, 2, KD, TOKENS], FP32, kind="Internal").ap()
    ctx = ExitStack()
    with ctx:
        def sb(name, shape, dt=FP32, where=ctx):
            return where.enter_context(nc.sbuf_tensor(name, shape, dt))

        bank = [ctx.enter_context(nc.psum_tensor(f"bank{i}", [P, 512], FP32)) for i in range(8)]
        keep = dict(
            ident=sb("ident", [P, P]),
            xs=sb("xs", [P, 2, KD, SEQ], FP32R),
            z=sb("z", [P, TILES, DIM]),
            s_zst=ctx.enter_context(nc.semaphore("z_stored")),
            s_xs=ctx.enter_context(nc.semaphore("tokens_loaded")),
            minus_half=sb("minus_half", [P, TILES]),
            wa_h=sb("wa_h", [P, KD, LATENT], FP32R),
            wa_l=sb("wa_l", [P, KD, LATENT], FP32R),
            wq_h=sb("wq_h", [P, 2, HEADS * HW], FP32R),
            wq_l=sb("wq_l", [P, 2, HEADS * HW], FP32R),
            wo_h=sb("wo_h", [P, PAIRS, DIM], FP32R),
            wo_l=sb("wo_l", [P, PAIRS, DIM], FP32R),
            warm=sb("warm", [P, 1]),
            b1t=sb("b1t", [P, EXPERTS * FT]),
        )
        with ExitStack() as two:
            xt_h = two.enter_context(nc.sbuf_tensor("xt_h", [P, KD, TOKENS], FP32R))
            xt_l = two.enter_context(nc.sbuf_tensor("xt_l", [P, KD, TOKENS], FP32R))
            pre = dict(
                w1_in=sb("w1_in", [P, 2, KD, FF], where=two),
                w2_in=sb("w2_in", [P, FT, DIM], where=two),
                b2_in=sb("b2_in", [P, 2, DIM], where=two),
                s_w1=two.enter_context(nc.semaphore("w1_loaded")),
                s_w2=two.enter_context(nc.semaphore("w2_loaded")),
                s_b2=two.enter_context(nc.semaphore("b2_loaded")),
            )
            with ExitStack() as own:
                prepare(nc, own, bank, keep, pre, xt_h, xt_l, x, q_a_w, q_a_ln, q_b_w, kv_a_w, kv_a_ln, kv_b_w, o_w,
                        b1, w1, w2, b2)
            with ExitStack() as own:
                experts(nc, own, bank, keep, pre, xt_h, xt_l, xt_dram, z_dram, w1, w2, b2)
        with ExitStack() as own:
            attend(nc, own, bank, keep, xt_dram, z_dram, x, cos_t, sin_t, out)


def prepare(nc, own, bank, keep, pre, xt_h, xt_l, x, q_a_w, q_a_ln, q_b_w, kv_a_w, kv_a_ln, kv_b_w, o_w, b1, w1,
            w2, b2):
    assert BATCH == PAIRS

    def sb(name, shape, dt=FP32):
        return own.enter_context(nc.sbuf_tensor(name, shape, dt))

    def sem(name):
        return own.enter_context(nc.semaphore(name))

    ident, minus_half = keep["ident"], keep["minus_half"]
    x_in = sb("x_in", [P, 2, TILES, DIM])
    xn = sb("xn", [P, TILES, DIM])
    stats = sb("stats", [P, TILES, 6])
    mean_var = sb("mean_var", [P, TILES, 2])
    rstd = sb("rstd", [P, TILES])
    wa_in = sb("wa_in", [P, 3, DIM])
    b1_in = sb("b1_in", [EXPERTS * FT, P])
    q_ln = sb("q_ln", [P, 2])
    kv_ln = sb("kv_ln", [P, KV_LORA])
    wqn = sb("wqn", [P, 2, 2, Q_LORA])
    wqr = sb("wqr", [ROPE, 2, 2, Q_LORA])
    wkv = sb("wkv", [P, 2, 2, 2, KV_LORA])
    wo_in = sb("wo_in", [P, 2, KD, 2 * VDIM])
    wot = sb("wot", [P, 2, 2, DIM])
    norm_bank = [bank[0:2], bank[2:4]]
    query_bank, turn_bank, output_bank = bank[4:6], bank[6], bank[7]
    GAINS, SMALL = 4, 5
    PW = 2 * HW

    s_x = [sem("x_loaded_even"), sem("x_loaded_odd")]
    s_w = [sem("pair_weights_loaded_even"), sem("pair_weights_loaded_odd")]
    s_gains = sem("gains_loaded")
    s_small = sem("down_projections_and_bias_loaded")
    s_const = sem("constants_made")
    s_dve = sem("statistics_ready")
    s_var = sem("variance_ready")
    s_eps = sem("eps_added")
    s_rstd = sem("rstd_ready")
    s_xn = sem("xn_ready")
    s_tr = sem("transposes_done")
    s_hi = sem("transpose_hi_copied")
    s_lo = sem("transpose_lo_copied")
    s_passed = sem("waits_passed")
    s_gain = sem("gain_applied")
    s_query = sem("query_weights_made")
    s_query_hi = sem("query_weights_hi_copied")
    s_query_free = sem("query_bank_free")
    s_turned = sem("output_weights_turned")
    s_wot = sem("turned_output_weights_copied")
    s_output = sem("output_weights_made")
    s_output_hi = sem("output_weights_hi_copied")
    s_output_free = sem("output_bank_free")
    s_job = sem("down_projection_or_bias_turned")
    s_job_hi = sem("down_projection_hi_copied")
    s_job_free = sem("down_projection_split")

    q_b_rows = q_b_w.rearrange("(h f) r -> f h r", f=QK)
    kv_b_rows = kv_b_w.rearrange("(h v p) r -> p h v r", v=2, p=P)
    o_rows = o_w.rearrange("(t p) n -> p t n", p=P)

    def steps(engine, step, between=None):
        with engine.Fori(0, BATCH // 2 - 1) as i:
            for odd in range(2):
                step(2 * i + odd, odd, False)
        step(BATCH - 2, 0, False)
        if between is not None:
            between()
        step(BATCH - 1, 1, True)

    def down_bank(n):
        return (query_bank[1], turn_bank, output_bank)[n]

    with nc.Block() as block:

        @block.sync
        def _(sp):
            def step(b, odd, last):
                sp.wait_ge(s_xn, b + 1)
                sp.dma_start(x_in[:, odd], x[bass.ds(b * SEQ, SEQ), :].rearrange("(t p) d -> p t d", p=P)) \
                    .then_inc(s_x[odd], 16)
                sp.wait_ge(s_output, b + 1)
                pair = bass.ds(2 * b, 2)
                sp.dma_start(wqn[:, odd], q_b_rows[0:NOPE, pair]).then_inc(s_w[odd], 16)
                sp.dma_start(wqr[:, odd], q_b_rows[NOPE:QK, pair]).then_inc(s_w[odd], 16)
                sp.dma_start(wkv[:, odd], kv_b_rows[:, pair]).then_inc(s_w[odd], 16)
                sp.dma_start(wo_in[:, odd], o_rows[:, :, bass.ds(b * 2 * VDIM, 2 * VDIM)]).then_inc(s_w[odd], 16)

            steps(sp, step)
            sp.dma_start(pre["w1_in"][:, 0], w1.rearrange("e (k p) f -> p e k f", p=P)[:, 0]).then_inc(pre["s_w1"], 16)
            sp.dma_start(pre["w2_in"][:, :, :], w2.rearrange("e (k p) n -> p e k n", p=P)[:, 0]) \
                .then_inc(pre["s_w2"], 16)
            for e in range(2):
                sp.dma_start(pre["b2_in"][:, e, :], b2[e, :].unsqueeze(0).to_broadcast([P, DIM])) \
                    .then_inc(pre["s_b2"], 16)

        @block.gpsimd
        def _(pool):
            pool.memset(ident[:], 0.0).then_inc(s_const, 1)
            pool.memset(minus_half[:], -0.5).then_inc(s_const, 1)
            pool.wait_ge(s_const, 2)
            pool.affine_select(out=ident[:], in_=ident[:], compare_op=ALU.not_equal, fill=1.0, base=0,
                               pattern=[[-1, P]], channel_multiplier=1).then_inc(s_const, 1)

            def norm(b):
                pool.wait_ge(s_var, b + 1)
                pool.sem_inc(s_passed, 1)
                pool.tensor_scalar(rstd[:], mean_var[:, :, 1], LN_EPS, None, ALU.add).then_inc(s_eps, 1)
                pool.wait_ge(s_eps, b + 1)
                pool.tensor_tensor(rstd[:], rstd[:], minus_half[:, 0:TILES], ALU.pow).then_inc(s_rstd, 1)

            def gain(b, odd):
                pool.wait_ge(s_gains, 16 * GAINS)
                pool.wait_ge(s_w[odd], 64 * (b // 2 + 1))
                w = wkv[:, odd].rearrange("p h v r -> p (h v) r")
                pool.tensor_tensor(w, w, kv_ln[:, :].unsqueeze(1).to_broadcast([P, 4, KV_LORA]),
                                   ALU.mult).then_inc(s_gain, 1)

            def step(b, odd, last):
                if not last:
                    gain(b + 1, 1 - odd)
                    norm(b + 1)

            norm(0)
            gain(0, 0)
            steps(pool, step)

        @block.scalar
        def _(act):
            small = (
                (q_ln[:, 0:1], q_a_ln[0:P].unsqueeze(1)),
                (q_ln[0:64, 1:2], q_a_ln[P:Q_LORA].unsqueeze(1)),
                (q_ln[64:P, 1:2], q_a_ln[P:Q_LORA].unsqueeze(1)),
                (kv_ln[:, :], kv_a_ln.unsqueeze(0).to_broadcast([P, KV_LORA])),
                (wa_in[:, 0, :], q_a_w[0:P, :]),
                (wa_in[0:Q_LORA - P, 1, :], q_a_w[P:Q_LORA, :]),
                (wa_in[Q_LORA - P:P, 1, :], kv_a_w[0:KV_LORA, :]),
                (wa_in[0:ROPE, 2, :], kv_a_w[KV_LORA:KV_LORA + ROPE, :]),
                (b1_in[:, :], b1.rearrange("e (k p) -> (e k) p", p=P)),
            )
            assert len(small) == GAINS + SMALL
            for n, (dst, src) in enumerate(small):
                act.dma_start(dst, src).then_inc(s_gains if n < GAINS else s_small, 16)
            act.wait_ge(s_gains, 16 * GAINS)

            def step(b, odd, last):
                act.wait_ge(s_query, b + 1)
                for i in range(2):
                    ins = act.activation(keep["wq_h"][:, i, bass.ds(b * PW, PW)],
                                         query_bank[odd][:, i * PW:(i + 1) * PW], ACT.Copy, scale=q_ln[:, i:i + 1])
                ins.then_inc(s_query_hi, 1)
                act.wait_ge(s_turned, b + 1)
                act.copy(wot[:, odd, :, :], turn_bank[:, :].rearrange("p (h n) -> p h n", h=2)) \
                    .then_inc(s_wot, 1)
                for k in range(KD):
                    act.wait_ge(s_tr, KD * b + k + 1)
                    act.copy(xt_h[:, k, bass.ds(b * SEQ, SEQ)], norm_bank[odd][k][:, :]).then_inc(s_hi, 1)
                act.wait_ge(s_output, 2 + b + 1)
                act.activation(keep["wo_h"][:, bass.ds(b, 1), :], output_bank[:, 0:DIM].unsqueeze(1), ACT.Copy,
                               scale=OUT_SCALE).then_inc(s_output_hi, 1)

            def down():
                for k in range(KD):
                    act.wait_ge(s_job, k + 1)
                    act.copy(keep["wa_h"][:, k, :], down_bank(k)[:, 0:LATENT]).then_inc(s_job_hi, 1)

            steps(act, step, down)

        @block.vector
        def _(dve):
            for free, count in ((s_xn, 2), (s_lo, 2 * KD), (s_query_free, 2), (s_output, 2), (s_wot, 1),
                                (s_output_free, 1)):
                dve.sem_inc(free, count)

            def statistics(b, odd):
                dve.wait_ge(s_x[odd], 16 * (b // 2 + 1))
                for t in range(TILES):
                    ins = dve.bn_stats(stats[:, t, :], x_in[:, odd, t, :])
                ins.then_inc(s_dve, 1)
                dve.wait_ge(s_dve, b + 1)
                dve.sem_inc(s_passed, 1)
                for t in range(TILES):
                    ins = dve.bn_aggr(mean_var[:, t, :], stats[:, t, :])
                ins.then_inc(s_var, 1)

            def step(b, odd, last):
                dve.wait_ge(s_var, b + 1)
                dve.wait_ge(s_rstd, b + 1)
                for t in range(TILES):
                    ins = dve.tensor_scalar(xn[:, t, :], x_in[:, odd, t, :], mean_var[:, t, 0:1], rstd[:, t:t + 1],
                                            ALU.subtract, ALU.mult)
                ins.then_inc(s_xn, 1)
                if not last:
                    statistics(b + 1, 1 - odd)
                dve.wait_ge(s_query_hi, b + 1)
                for i in range(2):
                    cols = bass.ds(b * PW, PW)
                    ins = dve.scalar_tensor_tensor(keep["wq_l"][:, i, cols], query_bank[odd][:, i * PW:(i + 1) * PW],
                                                   q_ln[:, i:i + 1], fp(keep["wq_h"][:, i, cols]), ALU.mult,
                                                   ALU.subtract)
                ins.then_inc(s_query_free, 1)
                for k in range(KD):
                    dve.wait_ge(s_hi, KD * b + k + 1)
                    dve.tensor_tensor(xt_l[:, k, bass.ds(b * SEQ, SEQ)], norm_bank[odd][k][:, :],
                                      fp(xt_h[:, k, bass.ds(b * SEQ, SEQ)]), ALU.subtract).then_inc(s_lo, 1)
                dve.wait_ge(s_output_hi, b + 1)
                dve.scalar_tensor_tensor(keep["wo_l"][:, bass.ds(b, 1), :], output_bank[:, 0:DIM].unsqueeze(1),
                                         OUT_SCALE, fp(keep["wo_h"][:, bass.ds(b, 1), :]), ALU.mult,
                                         ALU.subtract).then_inc(s_output_free, 1)

            def down():
                for k in range(KD):
                    dve.wait_ge(s_job_hi, k + 1)
                    dve.tensor_tensor(keep["wa_l"][:, k, :], down_bank(k)[:, 0:LATENT], fp(keep["wa_h"][:, k, :]),
                                      ALU.subtract).then_inc(s_job_free, 1)
                dve.wait_ge(s_job, KD + 1)
                dve.tensor_copy(keep["b1t"][:, :], down_bank(KD)[:, 0:EXPERTS * FT]).then_inc(s_job_free, 1)

            statistics(0, 0)
            dve.wait_ge(s_gains, 16 * GAINS)
            steps(dve, step, down)

        @block.tensor
        def _(pe):
            def step(b, odd, last):
                pe.wait_ge(s_w[odd], 64 * (b // 2 + 1))
                pe.wait_ge(s_gain, b + 1)
                pe.wait_ge(s_query_free, b + 1)
                if last:
                    pe.wait_ge(s_job_free, KD + 1)
                for i, rows, out_rows in ((0, slice(0, P), slice(0, P)), (1, slice(P, Q_LORA), slice(0, 64)),
                                          (1, slice(P, Q_LORA), slice(64, P))):
                    for hh in range(2):
                        c = i * PW + hh * HW
                        pe.matmul(query_bank[odd][out_rows, c:c + KV_LORA], wqn[:, odd, hh, rows],
                                  wkv[:, odd, hh, 0, :], start=True, stop=True)
                        turned = query_bank[odd][out_rows, c + KV_LORA:c + HW]
                        if out_rows.start == 0:
                            ins = pe.transpose(turned, wqr[:, odd, hh, rows], ident[0:ROPE, 0:ROPE])
                        else:
                            ins = pe.matmul(turned, wqr[:, odd, hh, rows], ident[0:ROPE, 0:ROPE], start=True, stop=True)
                ins.then_inc(s_query, 1)
                pe.wait_ge(s_wot, b + 1)
                for hh in range(2):
                    for k in range(KD):
                        ins = pe.transpose(turn_bank[:, hh * DIM + k * P:hh * DIM + (k + 1) * P],
                                           wo_in[:, odd, k, hh * VDIM:(hh + 1) * VDIM], ident[:, :])
                ins.then_inc(s_turned, 1)
                pe.wait_ge(s_xn, 2 + b + 1)
                for k in range(KD):
                    pe.wait_ge(s_lo, KD * b + k + 1)
                    for t in range(TILES):
                        ins = pe.transpose(norm_bank[odd][k][:, t * P:(t + 1) * P], xn[:, t, k * P:(k + 1) * P],
                                           ident[:, :])
                    ins.then_inc(s_tr, 1)
                pe.wait_ge(s_wot, 1 + b + 1)
                pe.wait_ge(s_output_free, b + 1)
                for hh in range(2):
                    ins = pe.matmul(output_bank[hh * 64:hh * 64 + 64, 0:DIM], wkv[:, odd, hh, 1, :],
                                    wot[:, odd, hh, :], start=True, stop=True)
                ins.then_inc(s_output, 1)

            def down():
                pe.wait_ge(s_small, 16 * SMALL)
                pe.wait_ge(s_query_free, 2 + BATCH - 2)
                for k in range(KD):
                    if k == 1:
                        pe.wait_ge(s_wot, 1 + BATCH - 1)
                    for i, rows in enumerate((P, P, ROPE)):
                        ins = pe.transpose(down_bank(k)[:, i * P:i * P + rows], wa_in[0:rows, i, k * P:(k + 1) * P],
                                           ident[0:rows, 0:rows])
                    ins.then_inc(s_job, 1)
                pe.wait_ge(s_output_free, 1 + BATCH - 1)
                pe.transpose(down_bank(KD)[:, 0:EXPERTS * FT], b1_in[:, :], ident[0:EXPERTS * FT, 0:EXPERTS * FT]) \
                    .then_inc(s_job, 1)

            pe.wait_ge(s_const, 3)
            steps(pe, step, down)


def experts(nc, own, bank, keep, pre, xt_h, xt_l, xt_dram, z_dram, w1, w2, b2):
    def sb(name, shape, dt=FP32):
        return own.enter_context(nc.sbuf_tensor(name, shape, dt))

    def sem(name):
        return own.enter_context(nc.semaphore(name))

    w1_in, w2_in, b2_in = pre["w1_in"], pre["w2_in"], pre["b2_in"]
    w1_h, w1_l = sb("w1_h", [P, KD, FF], FP32R), sb("w1_l", [P, KD, FF], FP32R)
    w2_h, w2_l = sb("w2_h", [P, FT, DIM], FP32R), sb("w2_l", [P, FT, DIM], FP32R)
    gelu = sb("gelu", [P, 2, CAP * BATCH])
    act_h = sb("act_h", [P, 4, CAP * BATCH], FP32R)
    act_l = sb("act_l", [P, 4, CAP * BATCH], FP32R)
    z = keep["z"]
    up = bank[0:4]
    down = bank[4:8]
    LAG = 2

    s_w1, s_w2, s_b2 = pre["s_w1"], pre["s_w2"], pre["s_b2"]
    s_xt_first = sem("first_tokens_stored")
    s_xt = sem("tokens_stored")
    s_w1h = sem("w1_hi_made")
    s_w2h = sem("w2_hi_made")
    s_w1s = sem("w1_split")
    s_w2s = sem("w2_split")
    s_up = sem("up_product_done")
    s_gelu = sem("gelu_done")
    s_act = sem("activation_split")
    s_act_h = sem("activation_hi_made")
    s_down = sem("down_product_step_done")
    s_z = sem("z_ready")
    s_zst = keep["s_zst"]

    w1_rows = w1.rearrange("e (k p) f -> p e k f", p=P)
    w2_rows = w2.rearrange("e (k p) n -> p e k n", p=P)
    z_rows = z_dram.rearrange("(q o e c) d -> o c e q d", o=2, e=EXPERTS, c=CAP)

    with nc.Block() as block:

        @block.sync
        def _(sp):
            sp.wait_ge(s_w1, 16)
            sp.dma_start(w1_in[:, 1], w1_rows[:, 1]).then_inc(s_w1, 16)
            sp.wait_ge(s_w2s, FT)
            sp.dma_start(w2_in[:, :, :], w2_rows[:, 1]).then_inc(s_w2, 16)
            sp.sem_inc(s_zst, 32)

            def load(e):
                sp.wait_ge(s_w1, 16 * (e + 2))
                sp.wait_ge(s_w1s, FT * (e + 1))
                sp.dma_start(w1_in[:, bass.ds(e % 2, 1)].rearrange("p o k f -> p (o k) f"),
                             w1_rows[:, bass.ds((e + 2) % EXPERTS, 1)].rearrange("p e k f -> p (e k) f")) \
                    .then_inc(s_w1, 16)
                sp.wait_ge(s_w2s, FT * (e + 2))
                sp.dma_start(w2_in[:, :, :], w2_rows[:, bass.ds((e + 2) % EXPERTS, 1)]
                             .rearrange("p e k n -> p (e k) n")).then_inc(s_w2, 16)

            def store_tokens(b, stored):
                for part, xt in enumerate((xt_h, xt_l)):
                    sp.dma_start(xt_dram[:, part, :, bass.ds(b * SEQ, SEQ)], fp(xt[:, :, bass.ds(b * SEQ, SEQ)])) \
                        .then_inc(stored, 16)

            def store(e):
                sp.wait_ge(s_z, TILES * (e + 2))
                for o in range(2):
                    sp.dma_start(z_rows[o][:, bass.ds(e, 1)].rearrange("c e q d -> c (e q) d"),
                                 z[o * CAP:(o + 1) * CAP, :, :]).then_inc(s_zst, 16)

            store_tokens(0, s_xt_first)
            with sp.Fori(0, EXPERTS - 1) as e:
                load(e)
                store_tokens(e + 1, s_xt)
                store(e)
                sp.dma_start(b2_in[:, bass.ds(e % 2, 1), :],
                             b2[bass.ds((e + 2) % EXPERTS, 1), :].unsqueeze(0).to_broadcast([P, 1, DIM])) \
                    .then_inc(s_b2, 16)
            sp.wait_ge(s_xt_first, 32)
            for part in range(2):
                sp.dma_start(fp(keep["xs"][:, part, :, :]), xt_dram[:, part, :, 0:SEQ]).then_inc(keep["s_xs"], 16)
            store(EXPERTS - 1)
            sp.wait_ge(s_w1, 16 * (EXPERTS + 1))
            sp.wait_ge(s_w2, 16 * (EXPERTS + 1))
            sp.wait_ge(s_xt, 32 * (BATCH - 1))
            sp.wait_ge(s_b2, 16 * (EXPERTS + 1))

        def w1_tile(w, k):
            return w[:, :, k * P:(k + 1) * P]

        def w1_loaded(e, k):
            return w1_in[:, bass.ds(e % 2, 1), :, k * P:(k + 1) * P]

        @block.scalar
        def _(act):
            def split_w1(e, k):
                act.wait_ge(s_w1, 16 * (e + 1))
                act.copy(w1_tile(w1_h, k).unsqueeze(1), w1_loaded(e, k)).then_inc(s_w1h, 1)

            def split_w2(loads, k):
                act.wait_ge(s_w2, 16 * loads)
                act.copy(w2_h[:, k, :], w2_in[:, k, :]).then_inc(s_w2h, 1)

            act.sem_inc(s_gelu, 4)
            for k in range(FT):
                split_w1(0, k)
            for k in range(FT):
                split_w2(1, k)
            with act.Fori(0, EXPERTS) as e:
                act.activation(keep["warm"][:, :], keep["minus_half"][:, 0:1], ACT.Gelu)
                for k in range(FT + LAG + 1):
                    if k < FT:
                        act.wait_ge(s_up, FT * e + k + 1)
                        act.wait_ge(s_act, FT * e + k + 1)
                        act.activation(gelu[:, k % 2, :], up[k % 4][:, :], ACT.Gelu,
                                       bias=keep["b1t"][:, bass.ds(e * FT + k, 1)]).then_inc(s_gelu, 1)
                        split_w1(e + 1, k)
                    if k > LAG:
                        act.wait_ge(s_down, 4 + FT * e + k - LAG)
                        split_w2(e + 2, k - LAG - 1)

        @block.vector
        def _(dve):
            def split_w1(e, k):
                dve.wait_ge(s_w1h, FT * e + k + 1)
                dve.tensor_tensor(w1_tile(w1_l, k).unsqueeze(1), w1_loaded(e, k), fp(w1_tile(w1_h, k)).unsqueeze(1),
                                  ALU.subtract).then_inc(s_w1s, 1)

            def split_w2(done, k):
                dve.wait_ge(s_w2h, done + k + 1)
                dve.tensor_tensor(w2_l[:, k, :], w2_in[:, k, :], fp(w2_h[:, k, :]),
                                  ALU.subtract).then_inc(s_w2s, 1)

            dve.sem_inc(s_act, 2)
            dve.sem_inc(s_z, TILES)
            for k in range(FT):
                split_w1(0, k)
            for k in range(FT):
                split_w2(0, k)
            with dve.Fori(0, EXPERTS) as e:
                for k in range(FT + LAG + 1):
                    if k < FT:
                        dve.wait_ge(s_gelu, 4 + FT * e + k + 1)
                        dve.wait_ge(s_down, FT * e + k + 1)
                        dve.tensor_copy(act_h[:, k % 4, :], gelu[:, k % 2, :]).then_inc(s_act_h, 1)
                        dve.wait_ge(s_act_h, FT * e + k + 1)
                        dve.tensor_tensor(act_l[:, k % 4, :], gelu[:, k % 2, :], fp(act_h[:, k % 4, :]),
                                          ALU.subtract).then_inc(s_act, 1)
                        split_w1(e + 1, k)
                    if k > LAG:
                        split_w2(FT * (e + 1), k - LAG - 1)
                dve.wait_ge(s_down, 4 + FT * (e + 1))
                dve.wait_ge(s_zst, 32 * (e + 1))
                dve.wait_ge(s_b2, 16 * (e + 2))
                for t in range(TILES):
                    dve.tensor_tensor(z[:, t:t + 1, :], down[t][:, 0:DIM].unsqueeze(1),
                                      b2_in[:, bass.ds(e % 2, 1), :], ALU.add).then_inc(s_z, 1)

        @block.tensor
        def _(pe):
            pe.sem_inc(s_down, 4)
            x_h = xt_h[:, :, :].rearrange("p k (b s) -> p k b s", s=SEQ)
            x_l = xt_l[:, :, :].rearrange("p k (b s) -> p k b s", s=SEQ)
            with pe.Fori(0, EXPERTS) as e:
                for k in range(FT + LAG):
                    if k < FT:
                        pe.wait_ge(s_w1s, FT * e + k + 1)
                        pe.wait_ge(s_gelu, FT * e + k + 1)
                        ps = up[k % 4][:, :].rearrange("p (b c) -> p b c", c=CAP)
                        n = 0
                        for d in range(KD):
                            for w, xx in ((w1_h, x_h), (w1_l, x_h), (w1_h, x_l)):
                                ins = pe.matmul(ps, w[:, d, k * P:(k + 1) * P], xx[:, d, :, bass.ds(e * CAP, CAP)],
                                                start=(n == 0), stop=(n == 3 * KD - 1))
                                n += 1
                        ins.then_inc(s_up, 1)
                    if k >= LAG:
                        j = k - LAG
                        pe.wait_ge(s_act, 2 + FT * e + j + 1)
                        pe.wait_ge(s_w2s, FT * e + j + 1)
                        if j == 0:
                            pe.wait_ge(s_z, TILES * (e + 1))
                        for t in range(TILES):
                            cols = slice(t * P, (t + 1) * P)
                            n = 0
                            for a, w in ((act_h, w2_h), (act_h, w2_l), (act_l, w2_h)):
                                ins = pe.matmul(down[t][:, 0:DIM], a[:, j % 4, cols], w[:, j, :],
                                                start=(j == 0 and n == 0), stop=(j == FT - 1 and n == 2))
                                n += 1
                        ins.then_inc(s_down, 1)


def attend(nc, own, bank, keep, xt_dram, z_dram, x, cos_t, sin_t, out):
    def sb(name, shape, dt=FP32):
        return own.enter_context(nc.sbuf_tensor(name, shape, dt))

    def sem(name):
        return own.enter_context(nc.semaphore(name))

    ident, xs, s_xs = keep["ident"], keep["xs"], keep["s_xs"]

    cos, sin = sb("cos", [P, TILES, ROPE]), sb("sin", [P, TILES, ROPE])
    mask = sb("mask", [P, SEQ])
    raw = sb("raw", [P, 2, LATENT])
    mean_sq = sb("mean_sq", [P, 2, 2])
    rms = sb("rms", [P, 2, 2])
    q_lat = sb("q_lat", [P, 2, 2 * P])
    keys = sb("keys", [P, 2, HW])
    turn = sb("turn", [P, 2, 2, ROPE])
    qlt_h = sb("qlt_h", [P, 2, SEQ], FP32R)
    qlt_l = sb("qlt_l", [P, SEQ], FP32R)
    keyt_h = sb("keyt_h", [P, 2, SEQ], FP32R)
    keyt_l = sb("keyt_l", [P, 2, SEQ], FP32R)
    lat = sb("lat", [P, 2 * TILES, 2, KV_LORA], FP16)
    q_tok = sb("q_tok", [P, TILES, GH, HW])
    q_turn = sb("q_turn", [P, 2, GH, ROPE])
    qt_h = sb("qt_h", [P, 2, GH, SEQ], FP32R)
    qt_l = sb("qt_l", [P, 2, GH, SEQ], FP32R)
    scores = sb("scores", [P, 2, SEQ])
    neg_max = sb("neg_max", [P, 2])
    probs = sb("probs", [P, 4, SEQ])
    sums = sb("sums", [P, 2, TILES])
    inv_sums = sb("inv_sums", [P, 2, TILES])
    pt_h = sb("pt_h", [P, 4, TILES, P], FP16)
    pt_l = sb("pt_l", [P, 4, TILES, P], FP16)
    mixed = sb("mixed", [P, 2, TILES, 2 * KV_LORA])
    mt_h = sb("mt_h", [P, PAIRS, SEQ], FP32R)
    mt_l = sb("mt_l", [P, PAIRS, SEQ], FP32R)
    x_res = sb("x_res", [P, TILES, DIM])
    gate = sb("gate", [P, TILES, DIM])
    result = sb("result", [P, TILES, DIM])

    score_bank, turned_bank, mix_bank, work_bank = bank[0:2], bank[2:4], bank[4:6], bank[6:8]
    out_bank = bank[0:4]

    s_rope = sem("rotation_tables_loaded")
    s_mask = sem("mask_made")
    s_res = sem("residual_and_gate_loaded")
    s_tanh = sem("tanh_ready")
    s_result = sem("result_ready")
    s_stored = sem("result_stored")
    s_projected = sem("output_projected")
    s_projected_free = sem("output_bank_free")
    s_scores = sem("score_bank_ready")
    s_scores_free = sem("score_bank_free")
    s_probs = sem("probs_ready")
    s_turned = sem("probs_transposed")
    s_pt_h = sem("probs_hi_copied")
    s_pt = sem("probs_split")
    s_mix = sem("mix_step_done")
    s_inv = sem("inverse_sums_ready")
    s_mix_free = sem("mix_bank_free")
    s_work = sem("work_bank_ready")
    s_work_hi = sem("work_bank_copied_by_scalar")
    s_work_free = sem("work_bank_free")
    s_eps = sem("rms_eps_added")
    s_rms = sem("rms_ready")
    s_keys = sem("latents_normed")
    s_turn = sem("key_rotation_products_ready")
    s_split = sem("latents_hi_made")
    s_qturn = sem("query_rotation_products_ready")
    s_qtok = sem("queries_turned")
    s_passed = sem("waits_passed")

    NEXT = [("latent", 0), ("latent", 1), ("flip", 0), ("latent", 2), ("flip", 1), ("latent", 3), ("flip", 2),
            ("flip", 3)] + [("query", (0, t)) for t in range(TILES)] + [("queryT", (0, j)) for j in range(GH)]
    plan = {step: ("mixedT", j) for j, step in enumerate(MIXED_TURN_STEPS)}
    for g in range(1, GROUPS):
        for steps, kind in ((QUERY_STEPS[g - 1], "query"), (QUERY_TURN_STEPS[g - 1], "queryT")):
            for i, step in enumerate(steps):
                assert step not in plan
                plan[step] = (kind, (g, i))
    for step, job in NEXT_STEPS:
        assert step not in plan
        plan[step] = job

    def jobs_of(last):
        steps = [step for step in sorted(plan) if not (last and plan[step] in NEXT)]
        return ({step: (n, *plan[step]) for n, step in enumerate(steps)},
                [plan[step] for step in steps] + [("mixedT", PAIRS - 1)])

    BY_SCALAR = ("latent", "query")
    START_BANKS = bank
    assert all(job in plan.values() for job in NEXT)
    JOBS, FIRST = len(jobs_of(False)[1]), len(NEXT)
    LAG_E, LAG_T, LAG_L, LAG_M = 1, 3, 4, 5
    STEPS = UNITS + LAG_M + 1
    MIXED_STEPS = [TILES * h + LAG_M + 5 for h in range(HEADS - 1)] + [STEPS - 1]
    assert JOBS % 2 == 0 and FIRST % 2 == 0

    def vector_step(step):
        return step + (LATENT_DELAY if plan[step][0] == "latent" else 1)

    def freed_of(jobs):
        return sum(kind not in BY_SCALAR for kind, _ in jobs)

    def freed_first(n):
        return freed_of(NEXT[:n])

    def freed(b, n, order):
        return freed_of(NEXT) + freed_of(jobs_of(False)[1]) * b + freed_of(order[:n])

    def queries_freed(b, g, j, order):
        if g == 0:
            return freed(b, 0, order) - (GH - 1 - j)
        return freed(b, 1 + order.index(("queryT", (g, j))), order)

    for j in range(GH):
        made = jobs_of(False)[1]
        assert freed_of(made[made.index(("queryT", (0, j))) + 1:]) >= GH - 1 - j

    def queries_done(b, g):
        return TILES * (GROUPS * b + (g - 1) % GROUPS + 1)

    def keys_of(u):
        return (u % TILES + 1) * P

    def rotate(engine, job, done, t):
        engine.wait_ge(s_work_hi, job + 1)
        engine.wait_ge(s_qtok, done + t + 1)
        src = q_tok[:, t, :, KV_LORA:]
        engine.tensor_tensor(q_turn[:, 0], src, cos[:, t, :].unsqueeze(1).to_broadcast([P, GH, ROPE]), ALU.mult)
        engine.tensor_tensor(q_turn[:, 1].rearrange("p h (a f) -> p h a f", a=2),
                             src.rearrange("p h (a f) -> p h a f", a=2)[:, :, ::-1, :],
                             sin[:, t, :].rearrange("p (a f) -> p a f", a=2).unsqueeze(1)
                             .to_broadcast([P, GH, 2, ROPE // 2]), ALU.mult).then_inc(s_qturn, 1)
        engine.wait_ge(s_qturn, done + t + 1)
        engine.tensor_tensor(src, q_turn[:, 0], q_turn[:, 1], ALU.add).then_inc(s_qtok, 1)

    with nc.Block() as block:

        @block.sync
        def _(sp):
            sp.sem_inc(s_stored, 16)
            for table, values in ((cos, cos_t), (sin, sin_t)):
                sp.dma_start(table[:, :, :], values.rearrange("(t p) f -> p t f", p=P)).then_inc(s_rope, 16)
            sp.wait_ge(keep["s_zst"], 32 * (EXPERTS + 1))

            def batch(b, last):
                rows = bass.ds(b * SEQ, SEQ)
                sp.wait_ge(s_result, TILES * (b + 1))
                sp.dma_start(x_res[:, :, :], x[rows, :].rearrange("(t p) d -> p t d", p=P)).then_inc(s_res, 16)
                sp.dma_start(gate[:, :, :], z_dram[rows, :].rearrange("(t p) d -> p t d", p=P)).then_inc(s_res, 16)
                if not last:
                    sp.wait_ge(s_work, FIRST + JOBS * b)
                    for part in range(2):
                        sp.dma_start(fp(xs[:, part, :, :]), xt_dram[:, part, :, bass.ds((b + 1) * SEQ, SEQ)]) \
                            .then_inc(s_xs, 16)
                sp.wait_ge(s_result, TILES * (b + 2))
                sp.dma_start(out[rows, :].rearrange("(t p) d -> p t d", p=P), result[:, :, :]).then_inc(s_stored, 16)

            with sp.Fori(0, BATCH - 1) as b:
                batch(b, False)
            batch(BATCH - 1, True)
            sp.wait_ge(s_xs, 32 * BATCH)
            sp.wait_ge(s_stored, 16 * (BATCH + 1))

        @block.gpsimd
        def _(pool):
            def latent(job, done, t):
                pool.wait_ge(s_work_hi, job + 1)
                pool.sem_inc(s_passed, 1)
                pool.tensor_scalar(rms[:, t % 2, :], mean_sq[:, t % 2, :], RMS_EPS, None, ALU.add).then_inc(s_eps, 1)
                pool.wait_ge(s_eps, done + t + 1)
                pool.tensor_tensor(rms[:, t % 2, :], rms[:, t % 2, :], keep["minus_half"][:, 0:2],
                                   ALU.pow).then_inc(s_rms, 1)

            pool.memset(mask[:], 0.0).then_inc(s_mask, 1)
            pool.wait_ge(s_mask, 1)
            pool.affine_select(out=mask[:, SEQ - P:], in_=mask[:, SEQ - P:], compare_op=ALU.is_ge, fill=NEG,
                               base=0, pattern=[[-1, P]], channel_multiplier=1).then_inc(s_mask, 1)
            pool.sem_inc(s_qtok, 1)
            for n, (kind, at) in enumerate(NEXT):
                if kind == "latent":
                    latent(n, 0, at)
            pool.wait_ge(s_rope, 32)
            def batch(b, last):
                beside, order = jobs_of(last)
                for s in range(STEPS):
                    if s in beside:
                        n, kind, at = beside[s]
                        if kind == "latent":
                            latent(FIRST + JOBS * b + n, TILES * (b + 1), at)
                        elif kind == "query":
                            rotate(pool, FIRST + JOBS * b + n, queries_done(b, at[0]), at[1])
                pool.wait_ge(s_res, 32 * (b + 1))
                for t in range(TILES):
                    pool.wait_ge(s_projected_free, TILES * (b + 1) + t + 1)
                    pool.tensor_tensor(result[:, t, :], result[:, t, :], x_res[:, t, :], ALU.add).then_inc(s_result, 1)

            with pool.Fori(0, BATCH - 1) as b:
                batch(b, False)
            batch(BATCH - 1, True)

        @block.scalar
        def _(act):
            def take(index, ps, kind, at, par):
                act.wait_ge(s_work, index + 1)
                if kind == "latent":
                    act.copy(raw[:, at % 2, :], ps[:, 0:LATENT])
                    act.activation(q_lat[:, at % 2, 0:Q_LORA], ps[:, 0:Q_LORA], ACT.Square,
                                   scale=float(Q_LORA) ** -0.5, accum_out=mean_sq[:, at % 2, 0:1])
                    ins = act.activation(q_lat[:, at % 2, Q_LORA:], ps[:, Q_LORA:Q_LORA + KV_LORA], ACT.Square,
                                         scale=float(KV_LORA) ** -0.5, accum_out=mean_sq[:, at % 2, 1:2])
                elif kind == "flip":
                    cols = slice(at * P, (at + 1) * P)
                    act.copy(qlt_h[:, :, cols], ps[:, 0:2 * P].rearrange("p (a c) -> p a c", a=2))
                    ins = act.copy(keyt_h[:, bass.ds(par, 1), cols], ps[:, 2 * P:3 * P].unsqueeze(1))
                elif kind == "query":
                    g, t = at
                    ins = act.copy(q_tok[:, t, :, :], ps[:, :].rearrange("p (h f) -> p h f", h=GH))
                elif kind == "queryT":
                    g, j = at
                    ins = act.copy(qt_h[:, g % 2, j, :], ps[:, :])
                else:
                    ins = act.copy(mt_h[:, at, :], ps[:, :])
                ins.then_inc(s_work_hi, 1)

            act.sem_inc(s_probs, 2)
            for n, (kind, at) in enumerate(NEXT):
                take(n, START_BANKS[n % 8], kind, at, 0)
            def batch(b, last):
                beside, order = jobs_of(last)
                act.activation(keep["warm"][:, :], keep["minus_half"][:, 0:1], ACT.Exp)
                for s in range(STEPS):
                    u = s - LAG_T
                    if 0 <= u < UNITS:
                        act.wait_ge(s_turned, 4 + UNITS * b + u + 1)
                        act.wait_ge(s_mix, UNITS * b + u + 1)
                        m = u % TILES + 1
                        act.activation(pt_h[:, u % 4, 0:m, :],
                                       turned_bank[u % 2][:, 0:m * P].rearrange("p (m c) -> p m c", c=P),
                                       ACT.Copy, scale=P_SCALE).then_inc(s_pt_h, 1)
                    u = s - LAG_E
                    if 0 <= u < UNITS:
                        act.wait_ge(s_scores_free, 2 + UNITS * b + u + 1)
                        act.wait_ge(s_turned, UNITS * b + u + 1)
                        act.activation(probs[:, u % 4, 0:keys_of(u)], scores[:, u % 2, 0:keys_of(u)], ACT.Exp,
                                       scale=-1.0, bias=neg_max[:, u % 2:u % 2 + 1],
                                       accum_out=sums[:, u // TILES % 2, u % TILES:u % TILES + 1]) \
                            .then_inc(s_probs, 1)
                    if s in beside:
                        n, kind, at = beside[s]
                        take(FIRST + JOBS * b + n, work_bank[n % 2], kind, at, (b + 1) % 2)
                    if s == UNITS + 1:
                        act.wait_ge(s_res, 32 * (b + 1))
                        act.wait_ge(s_stored, 16 * (b + 1))
                        act.activation(result[:, :, :], gate[:, :, :], ACT.Tanh, scale=0.5).then_inc(s_tanh, 1)
                for n, (kind, at) in enumerate(order[len(beside):], len(beside)):
                    take(FIRST + JOBS * b + n, work_bank[n % 2], kind, at, None)

            with act.Fori(0, BATCH - 1) as b:
                batch(b, False)
            batch(BATCH - 1, True)

        @block.vector
        def _(dve):
            def take(index, ps, kind, at, par, lat_done):
                if kind == "latent":
                    t = at
                    dve.wait_ge(s_rms, lat_done + t + 1)
                    dve.wait_ge(s_split, lat_done + t + 1)
                    dve.tensor_scalar(q_lat[:, t % 2, 0:Q_LORA], raw[:, t % 2, 0:Q_LORA], rms[:, t % 2, 0:1], None,
                                      ALU.mult)
                    dve.tensor_scalar(q_lat[:, t % 2, Q_LORA:], raw[:, t % 2, P:Q_LORA], rms[:, t % 2, 0:1], None,
                                      ALU.mult)
                    dve.tensor_scalar(keys[:, t % 2, 0:KV_LORA], raw[:, t % 2, Q_LORA:Q_LORA + KV_LORA],
                                      rms[:, t % 2, 1:2], None, ALU.mult)
                    src = raw[:, t % 2, Q_LORA + KV_LORA:]
                    dve.tensor_tensor(turn[:, t % 2, 0, :], src, cos[:, t, :], ALU.mult)
                    dve.tensor_tensor(turn[:, t % 2, 1, :].rearrange("p (a f) -> p a f", a=2),
                                      src.rearrange("p (a f) -> p a f", a=2)[:, ::-1, :],
                                      sin[:, t, :].rearrange("p (a f) -> p a f", a=2),
                                      ALU.mult).then_inc(s_turn, 1)
                    dve.wait_ge(s_turn, lat_done + t + 1)
                    dve.tensor_tensor(keys[:, t % 2, KV_LORA:], turn[:, t % 2, 0, :], turn[:, t % 2, 1, :],
                                      ALU.add).then_inc(s_keys, 1)
                    row = bass.ds(par * TILES + t, 1)
                    src = keys[:, t % 2, 0:KV_LORA].unsqueeze(1)
                    dve.tensor_scalar(lat[:, row, 0, :], src, C_SCALE, None, ALU.mult).then_inc(s_split, 1)
                    dve.wait_ge(s_split, 1 + lat_done + t + 1)
                    dve.scalar_tensor_tensor(lat[:, row, 1, :], src, C_SCALE, lat[:, row, 0, :], ALU.mult,
                                             ALU.subtract)
                    return
                dve.wait_ge(s_work_hi, index + 1)
                if kind == "flip":
                    cols = slice(at * P, (at + 1) * P)
                    dve.tensor_tensor(qlt_l[:, cols], ps[:, 0:P], fp(qlt_h[:, 0, cols]), ALU.subtract)
                    dve.tensor_tensor(qlt_h[64:P, 1, cols], ps[64:P, P:2 * P], fp(qlt_h[64:P, 1, cols]),
                                      ALU.subtract)
                    ins = dve.tensor_tensor(keyt_l[:, bass.ds(par, 1), cols], ps[:, 2 * P:3 * P].unsqueeze(1),
                                            fp(keyt_h[:, bass.ds(par, 1), cols]), ALU.subtract)
                elif kind == "queryT":
                    g, j = at
                    ins = dve.tensor_tensor(qt_l[:, g % 2, j, :], ps[:, :], fp(qt_h[:, g % 2, j, :]), ALU.subtract)
                else:
                    ins = dve.tensor_tensor(mt_l[:, at, :], ps[:, :], fp(mt_h[:, at, :]), ALU.subtract)
                ins.then_inc(s_work_free, 1)

            dve.wait_ge(s_rope, 32)
            for free, count in ((s_scores_free, 2), (s_pt, 2), (s_mix_free, 2), (s_result, TILES),
                                (s_projected_free, TILES), (s_split, 1)):
                dve.sem_inc(free, count)
            for n, (kind, at) in enumerate(NEXT):
                if kind == "query":
                    rotate(dve, n, 0, at[1])
                else:
                    take(n, START_BANKS[n % 8], kind, at, 0, 0)
            dve.wait_ge(s_mask, 2)

            def batch(b, last):
                beside, order = jobs_of(last)

                def beside_step(s):
                    if s in beside and beside[s][1] != "query":
                        n, kind, at = beside[s]
                        take(FIRST + JOBS * b + n, work_bank[n % 2], kind, at, (b + 1) % 2, TILES * (b + 1))

                for s in range(STEPS):
                    u = s - LAG_L
                    if 0 <= u < UNITS:
                        m = u % TILES + 1
                        dve.wait_ge(s_pt_h, UNITS * b + u + 1)
                        dve.scalar_tensor_tensor(pt_l[:, u % 4, 0:m, :],
                                                 turned_bank[u % 2][:, 0:m * P].rearrange("p (m c) -> p m c", c=P),
                                                 P_SCALE, pt_h[:, u % 4, 0:m, :], ALU.mult,
                                                 ALU.subtract).then_inc(s_pt, 1)
                    if s in MIXED_STEPS:
                        h = MIXED_STEPS.index(s)
                        dve.wait_ge(s_mix, 4 + UNITS * b + TILES * (h + 1))
                        dve.wait_ge(s_inv, HEADS * b + h + 1)
                        dve.tensor_tensor(mixed[:, h // 2 % 2, :, h % 2 * KV_LORA:(h % 2 + 1) * KV_LORA],
                                          mix_bank[h % 2][:, 0:TILES * KV_LORA]
                                          .rearrange("p (t c) -> p t c", c=KV_LORA),
                                          inv_sums[:, h % 2, :].unsqueeze(2).to_broadcast([P, TILES, KV_LORA]),
                                          ALU.mult).then_inc(s_mix_free, 1)
                    if s < UNITS:
                        N = keys_of(s)
                        dve.wait_ge(s_scores, UNITS * b + s + 1)
                        dve.wait_ge(s_probs, UNITS * b + s + 1)
                        dve.sem_inc(s_passed, 1)
                        dve.tensor_tensor_reduce(out=scores[:, s % 2, 0:N], in0=score_bank[s % 2][:, 0:N],
                                                 in1=mask[:, SEQ - N:SEQ], scale=-SCALE, scalar=-NEG,
                                                 op0=ALU.add, op1=ALU.min,
                                                 accum_out=neg_max[:, s % 2:s % 2 + 1])\
                            .then_inc(s_scores_free, 1)
                    for step in range(STEPS):
                        if step in beside and vector_step(step) == s:
                            beside_step(step)
                    if s % TILES == 2 and 6 <= s < UNITS + 4:
                        h = (s - 6) // TILES
                        dve.wait_ge(s_probs, 2 + UNITS * b + TILES * (h + 1))
                        dve.reciprocal(inv_sums[:, h % 2, :], sums[:, h % 2, :]).then_inc(s_inv, 1)
                    if s == UNITS + 3:
                        dve.wait_ge(s_tanh, b + 1)
                        dve.scalar_tensor_tensor(gate[:, :, :], result[:, :, :], 1.0, gate[:, :, :], ALU.add, ALU.mult)

                for n, (kind, at) in enumerate(order[len(beside):], len(beside)):
                    take(FIRST + JOBS * b + n, work_bank[n % 2], kind, at, None, None)
                for t in range(TILES):
                    dve.wait_ge(s_projected, TILES * b + t + 1)
                    dve.tensor_tensor(result[:, t, :], out_bank[t][:, 0:DIM], gate[:, t, :],
                                      ALU.mult).then_inc(s_projected_free, 1)

            with dve.Fori(0, BATCH - 1) as b:
                batch(b, False)
            batch(BATCH - 1, True)

        @block.tensor
        def _(pe):
            def three(ps, parts):
                n = 0
                for (a_h, a_l), (w_h, w_l) in parts:
                    for a, w in ((a_h, w_h), (a_h, w_l), (a_l, w_h)):
                        ins = pe.matmul(ps, a, w, start=(n == 0), stop=(n == 3 * len(parts) - 1))
                        n += 1
                return ins

            def make(index, bank_free, ps, kind, at, lat_done, q_done, flipped, mixed_done=None):
                if bank_free is not None:
                    pe.wait_ge(*bank_free)
                if kind == "latent":
                    if at == 0:
                        pe.wait_ge(s_xs, 32 * (lat_done + 1))
                    cols = slice(at * P, (at + 1) * P)
                    ins = three(ps[:, 0:LATENT],
                                [((xs[:, 0, k, cols], xs[:, 1, k, cols]),
                                  (keep["wa_h"][:, k, :], keep["wa_l"][:, k, :])) for k in range(KD)])
                elif kind == "flip":
                    pe.wait_ge(s_keys, lat_done * TILES + at + 1)
                    pe.transpose(ps[:, 0:P], q_lat[:, at % 2, 0:P], ident[:, :])
                    pe.transpose(ps[:, P:2 * P], q_lat[:, at % 2, P:], ident[:, :])
                    ins = pe.transpose(ps[:, 2 * P:3 * P], keys[:, at % 2, :], ident[:, :])
                elif kind == "query":
                    g, t = at
                    if g == 0:
                        pe.wait_ge(s_work_free, flipped)
                    rows, cols = slice(t * P, (t + 1) * P), slice(g * GW, (g + 1) * GW)
                    wq_h, wq_l = keep["wq_h"], keep["wq_l"]
                    pairs = ((qlt_h[:, 0, rows], wq_h[:, 0, cols]), (qlt_h[:, 0, rows], wq_l[:, 0, cols]),
                             (qlt_l[:, rows], wq_h[:, 0, cols]),
                             (qlt_h[:, 1, rows], wq_h[:, 1, cols]), (qlt_h[:, 1, rows], wq_l[:, 1, cols]))
                    for i, (a, w) in enumerate(pairs):
                        ins = pe.matmul(ps[:, :], a, w, start=(i == 0), stop=(i == len(pairs) - 1))
                elif kind == "queryT":
                    g, j = at
                    if j == 0:
                        pe.wait_ge(s_qtok, 1 + q_done + TILES)
                    for t in range(TILES):
                        ins = pe.transpose(ps[:, t * P:(t + 1) * P], q_tok[:, t, j, :], ident[:, :])
                else:
                    pe.wait_ge(s_mix_free, mixed_done + 2 * at + 2)
                    for t in range(TILES):
                        ins = pe.transpose(ps[:, t * P:(t + 1) * P], mixed[:, at % 2, t, :], ident[:, :])
                ins.then_inc(s_work, 1)

            pe.sem_inc(s_turned, 4)
            pe.sem_inc(s_mix, 4)
            for n, (kind, at) in enumerate(NEXT):
                bank_free = None
                if n >= 8:
                    bank_free = (s_work_hi, n - 7) if NEXT[n - 8][0] in BY_SCALAR else (s_work_free, freed_first(n - 7))
                flipped = freed_first(1 + NEXT.index(("flip", at[1]))) if kind == "query" else None
                make(n, bank_free, START_BANKS[n % 8], kind, at, 0, 0, flipped)
            def batch(b, last):
                beside, order = jobs_of(last)
                def bank_free(n):
                    if n >= 2 and order[n - 2][0] in BY_SCALAR:
                        return s_work_hi, FIRST + JOBS * b + n - 1
                    return s_work_free, freed(b, n - 1, order) if n >= 1 else freed(b, 0, order) - 1

                def flipped(kind, at):
                    if kind == "query" and at[0] == 0:
                        return freed(b, 1 + order.index(("flip", at[1])), order)
                    return None

                def q_done(kind, at):
                    return queries_done(b, at[0]) if kind == "queryT" else None

                def project(t, pairs):
                    for j in pairs:
                        rows = slice(t * P, (t + 1) * P)
                        for i, (a, w) in enumerate(((mt_h, "wo_h"), (mt_h, "wo_l"), (mt_l, "wo_h"))):
                            ins = pe.matmul(out_bank[t][:, 0:DIM], a[:, j, rows], keep[w][:, j, :],
                                            start=(j == 0 and i == 0), stop=(j == PAIRS - 1 and i == 2))
                    return ins

                for s in range(STEPS):
                    if s < UNITS:
                        h, t = s // TILES, s % TILES
                        g, j = h // GH, h % GH
                        if t == 0:
                            pe.wait_ge(s_work_free, queries_freed(b, g, j, order))
                        if s < 2:
                            pe.wait_ge(s_projected_free, TILES * b + s + 1)
                        pe.wait_ge(s_scores_free, UNITS * b + s + 1)
                        N = max(keys_of(s), 2 * P)
                        rows = slice(t * P, (t + 1) * P)
                        par = bass.ds(b % 2, 1)
                        ps = score_bank[s % 2][:, 0:N].unsqueeze(1)
                        three(ps, [((qt_h[:, g % 2, j, rows], qt_l[:, g % 2, j, rows]),
                                    (keyt_h[:, par, 0:N], keyt_l[:, par, 0:N]))]).then_inc(s_scores, 1)
                    u = s - LAG_T
                    if 0 <= u < UNITS:
                        if u < 2:
                            pe.wait_ge(s_projected_free, TILES * b + 2 + u + 1)
                        pe.wait_ge(s_probs, 2 + UNITS * b + u + 1)
                        pe.wait_ge(s_pt, UNITS * b + u + 1)
                        for k in range(u % TILES + 1):
                            ins = pe.transpose(turned_bank[u % 2][:, k * P:(k + 1) * P],
                                               probs[:, u % 4, k * P:(k + 1) * P], ident[:, :])
                        ins.then_inc(s_turned, 1)
                    u = s - LAG_M
                    if 0 <= u < UNITS:
                        h, t = u // TILES, u % TILES
                        pe.wait_ge(s_pt, 2 + UNITS * b + u + 1)
                        if t == 0:
                            pe.wait_ge(s_mix_free, HEADS * b + h + 1)
                        for k in range(t + 1):
                            row = bass.ds(b % 2 * TILES + k, 1)
                            for i, (pt, part) in enumerate(((pt_h, 0), (pt_h, 1), (pt_l, 0))):
                                ins = pe.matmul(mix_bank[h % 2][:, t * KV_LORA:(t + 1) * KV_LORA].unsqueeze(1),
                                                pt[:, u % 4, k, :], lat[:, row, part, :],
                                                start=(k == 0 and i == 0), stop=(k == t and i == 2))
                        ins.then_inc(s_mix, 1)
                    if s in beside:
                        n, kind, at = beside[s]
                        make(FIRST + JOBS * b + n, bank_free(n), work_bank[n % 2], kind, at, b + 1, q_done(kind, at),
                             flipped(kind, at), 2 + HEADS * b)
                    t = s - (STEPS - TILES)
                    if t >= 0:
                        if t == 0:
                            pe.wait_ge(s_work_free, freed(b, 1 + order.index(("mixedT", PAIRS - 3)), order))
                        pe.wait_ge((s_scores_free, s_pt)[t // 2], 2 + UNITS * (b + 1) - 1 + t % 2)
                        project(t, range(PAIRS - 2))
                for n, (kind, at) in enumerate(order[len(beside):], len(beside)):
                    make(FIRST + JOBS * b + n, bank_free(n), work_bank[n % 2], kind, at, None, None, None,
                         2 + HEADS * b)
                pe.wait_ge(s_work_free, freed(b, len(order) - 1, order))
                for t in range(TILES):
                    project(t, [PAIRS - 2])
                pe.wait_ge(s_work_free, freed(b, len(order), order))
                for t in range(TILES):
                    project(t, [PAIRS - 1]).then_inc(s_projected, 1)

            with pe.Fori(0, BATCH - 1) as b:
                batch(b, False)
            batch(BATCH - 1, True)


_INS = ["L0_attn_hidden_states", "L0_attn_q_a_w", "L0_attn_q_a_ln_w", "L0_attn_q_b_w", "L0_attn_kv_a_w",
        "L0_attn_kv_a_ln_w", "L0_attn_kv_b_w", "L0_attn_o_w", "L0_ffn_w1", "L0_ffn_b1", "L0_ffn_w2", "L0_ffn_b2"]


def rope_tables():
    f32 = np.float32
    inv_freq = f32(1.0) / f32(ROPE_THETA) ** (np.arange(0, ROPE, 2, dtype=f32) / f32(ROPE))
    angle = np.outer(np.arange(SEQ, dtype=f32), inv_freq.astype(f32)).astype(f32)
    cos, sin = np.cos(angle), np.sin(angle)
    return (np.concatenate([cos, cos], axis=-1).astype(f32), np.concatenate([-sin, sin], axis=-1).astype(f32))


def kernel(**inputs):
    import concourse.bacc as bacc
    from concourse.bass_utils import run_bass_kernel_spmd

    nc = bacc.Bacc("TRN2", target_bir_lowering=False, num_devices=1)
    arrays = {name: np.ascontiguousarray(inputs[name]) for name in _INS}
    arrays["L0_attn_hidden_states"] = arrays["L0_attn_hidden_states"].reshape(TOKENS, DIM)
    arrays["cos_table"], arrays["sin_table"] = rope_tables()
    args = [nc.dram_tensor(f"in_{n}", a.shape, mybir.dt.from_np(a.dtype), kind="ExternalInput").ap()
            for n, a in arrays.items()]
    out = nc.dram_tensor("out", (TOKENS, DIM), FP32, kind="ExternalOutput").ap()
    build(nc, *args, out)
    r = run_bass_kernel_spmd(nc, [{f"in_{n}": a for n, a in arrays.items()}], core_ids=[0])
    return r.results[0]["out"].reshape(BATCH, SEQ, DIM)
```
